# Optimizing a Trainium2 kernel written in Bass

```python
import numpy as np
import jax
import jax.numpy as jnp

def _softmax(x, axis=-1):
    return jax.nn.softmax(x, axis=axis)

def _gelu(x):
    return jax.nn.gelu(x, approximate=True)

def _silu(x):
    return jax.nn.silu(x)

def _sigmoid(x):
    return jax.nn.sigmoid(x)

def _layernorm(x, axis=-1, eps=1e-05):
    m = jnp.mean(x, axis=axis, keepdims=True)
    v = jnp.var(x, axis=axis, keepdims=True)
    return (x - m) / jnp.sqrt(v + eps)

def _scatter_add(tgt, idx, src, axis=0):
    return tgt.at[idx].add(src)

def _segment_sum(src, seg, n):
    return jax.ops.segment_sum(src, seg, n)
kernel_name = 'mk_prb_d1_jaxref_r4_a417ac'

def setup_inputs(seed: int=0):
    np.random.seed(seed)
    _w = jnp.asarray

    def _L0_attn_setup():
        import jax, jax.numpy as jnp
        import numpy as np
        D_MODEL = 256
        N_HEAD = 16
        HEAD_DIM = D_MODEL // N_HEAD
        key = jax.random.key(seed)
        k1, k2, k3 = jax.random.split(key, 3)
        x = jax.random.normal(k1, (2, 512, D_MODEL), dtype=jnp.float32)
        w_in = jax.random.normal(k2, (3 * D_MODEL, D_MODEL), dtype=jnp.float32) * (1.0 / np.sqrt(D_MODEL))
        w_out = jax.random.normal(k3, (D_MODEL, D_MODEL), dtype=jnp.float32) * (1.0 / np.sqrt(D_MODEL))
        return {'x': x, 'w_in': w_in, 'w_out': w_out}
    _L0_attn_in = _L0_attn_setup()

    def _L0_ffn_setup():
        import jax, jax.numpy as jnp
        import numpy as np
        DIM = 256

        def _reference_tuple_inner(x, W_r, W_k, W_v, mu_r, mu_k):
            B, T, C = x.shape
            x_prev = jnp.concatenate([jnp.zeros((B, 1, C), x.dtype), x[:, :-1, :]], axis=1)
            xr = mu_r * x + (1.0 - mu_r) * x_prev
            xk = mu_k * x + (1.0 - mu_k) * x_prev
            r = jax.nn.sigmoid(jnp.einsum('btc,dc->btd', xr, W_r))
            k = jnp.einsum('btc,dc->btd', xk, W_k)
            k_act = jnp.square(jax.nn.relu(k))
            out = r * jnp.einsum('btc,dc->btd', k_act, W_v)
            new_state = x[:, -1, :]
            return (out, new_state)
        key = jax.random.key(seed)
        ks = jax.random.split(key, 6)
        B, T, C = (8, 512, DIM)
        x = jax.random.normal(ks[0], (B, T, C), dtype=jnp.float32)
        s = 1.0 / np.sqrt(C)
        W_r = jax.random.uniform(ks[1], (C, C), jnp.float32, -s, s)
        W_k = jax.random.uniform(ks[2], (C, C), jnp.float32, -s, s)
        W_v = jax.random.uniform(ks[3], (C, C), jnp.float32, -s, s)
        mu_r = jax.random.uniform(ks[4], (C,), jnp.float32)
        mu_k = jax.random.uniform(ks[5], (C,), jnp.float32)
        return {'x': x, 'W_r': W_r, 'W_k': W_k, 'W_v': W_v, 'mu_r': mu_r, 'mu_k': mu_k}
    _L0_ffn_in = _L0_ffn_setup()
    _d = {'L0_attn_x': _L0_attn_in['x'], 'L0_attn_w_in': _L0_attn_in['w_in'], 'L0_attn_w_out': _L0_attn_in['w_out'], 'L0_ffn_W_r': _L0_ffn_in['W_r'], 'L0_ffn_W_k': _L0_ffn_in['W_k'], 'L0_ffn_W_v': _L0_ffn_in['W_v'], 'L0_ffn_mu_r': _L0_ffn_in['mu_r'], 'L0_ffn_mu_k': _L0_ffn_in['mu_k']}
    _x0 = _d['L0_attn_x']
    _d['L0_attn_x'] = jax.random.normal(jax.random.fold_in(jax.random.key(seed), 1), (2, 2048, 256), dtype=_x0.dtype)
    del _x0
    return _d

def reference(L0_attn_x, L0_attn_w_in, L0_attn_w_out, L0_ffn_W_r, L0_ffn_W_k, L0_ffn_W_v, L0_ffn_mu_r, L0_ffn_mu_k):

    def _L0_attn_ref(x, w_in, w_out):
        import jax, jax.numpy as jnp
        import numpy as np
        D_MODEL = 256
        N_HEAD = 16
        HEAD_DIM = D_MODEL // N_HEAD
        B, T, D = x.shape
        qkv = jnp.einsum('btd,ed->bte', x, w_in)
        q, k, v = jnp.split(qkv, 3, axis=2)

        def heads(t):
            return t.reshape(B, T, N_HEAD, HEAD_DIM).transpose(0, 2, 1, 3)
        q, k, v = (heads(q), heads(k), heads(v))
        att = jnp.einsum('bhqd,bhkd->bhqk', q, k) / np.sqrt(HEAD_DIM).astype(np.float32)
        causal = jnp.tril(jnp.ones((T, T), dtype=bool))
        att = jnp.where(causal, att, 0.0)
        att = jax.nn.softmax(att, axis=-1)
        out = jnp.einsum('bhqk,bhkd->bhqd', att, v)
        out = out.transpose(0, 2, 1, 3).reshape(B, T, D)
        return jnp.einsum('btd,ed->bte', out, w_out)

    def _L0_ffn_ref(x, W_r, W_k, W_v, mu_r, mu_k):
        import jax, jax.numpy as jnp
        import numpy as np
        DIM = 256

        def _reference_tuple_inner(x, W_r, W_k, W_v, mu_r, mu_k):
            B, T, C = x.shape
            x_prev = jnp.concatenate([jnp.zeros((B, 1, C), x.dtype), x[:, :-1, :]], axis=1)
            xr = mu_r * x + (1.0 - mu_r) * x_prev
            xk = mu_k * x + (1.0 - mu_k) * x_prev
            r = jax.nn.sigmoid(jnp.einsum('btc,dc->btd', xr, W_r))
            k = jnp.einsum('btc,dc->btd', xk, W_k)
            k_act = jnp.square(jax.nn.relu(k))
            out = r * jnp.einsum('btc,dc->btd', k_act, W_v)
            new_state = x[:, -1, :]
            return (out, new_state)
        return _reference_tuple_inner(x, W_r, W_k, W_v, mu_r, mu_k)[0]
    x = L0_attn_x
    xn = _layernorm(x, axis=-1)
    x = x + _L0_attn_ref(xn, L0_attn_w_in, L0_attn_w_out) + _L0_ffn_ref(xn, L0_ffn_W_r, L0_ffn_W_k, L0_ffn_W_v, L0_ffn_mu_r, L0_ffn_mu_k)
    return x

_drawn_inputs = setup_inputs


def setup_inputs(seed=0):
    import zlib

    import numpy as np

    out = dict(_drawn_inputs(seed))
    spreads = {}
    factors = {'L0_ffn_W_r': 3.308, 'L0_ffn_mu_r': 6.652}
    for name, (base, spread) in spreads.items():
        noise = np.random.default_rng([zlib.crc32(name.encode()), seed]).standard_normal(out[name].shape)
        drawn = base * np.exp(spread * noise) if base else spread * noise
        out[name] = jnp.asarray(drawn.astype(out[name].dtype))
    for name, factor in factors.items():
        out[name] = (out[name] * factor).astype(out[name].dtype)
    return out
```

```python
from contextlib import ExitStack

import concourse.bass as bass
from concourse import mybir

F32 = mybir.dt.float32
BF16 = mybir.dt.bfloat16
ALU = mybir.AluOpType
ACT = mybir.ActivationFunctionType
AX_X = mybir.AxisListType.X

P = 128
B, T, C = 2, 2048, 256
H, HD = 16, 16
SCALE = 0.25
EPS = 1e-5
CC = C // P
CH = 512
NCH = T // CH
SUB = CH // P
NT = T // P
GH = 4
NG = H // GH
HW = 32
NEG = -1e30
LOWEST = -3e38

Q_PARTS = (0, 1, 2, 0, 1, 0)
K_PARTS = (0, 0, 0, 1, 1, 2)
ROWS = HD * len(Q_PARTS)
KROWS = ROWS + 3

PIECE0 = [SUB * GH * u * (u + 1) // 2 for u in range(NCH + 1)]
PIECES = PIECE0[NCH]
HEAD_START = PIECE0[2] + 32
SLOT_PIECES = {0: (HEAD_START, PIECE0[3]), 1: (PIECE0[3], PIECE0[3] + 24),
               2: (PIECE0[3] + 24, PIECES), 3: (0, HEAD_START)}
SLOT_SPREAD = {0: 8, 1: 16, 2: 16, 3: 32}
SHIFT_AT = {(3, 3): 0, (3, 6): 1, (1, 0): 2, (2, 4): 3}
SV_AT = {(3, 1): 0, (3, 2): 1, (3, 4): 2, (3, 5): 3}
STEPS = [2 * u + 2 for u in range(NCH)]
STEP0 = [sum(STEPS[:u]) for u in range(NCH + 1)]
GSTEPS = STEP0[NCH]
PRING = 8


def piece(f):
    u = max(v for v in range(NCH) if PIECE0[v] <= f)
    hs, pc = divmod(f - PIECE0[u], u + 1)
    h, s = divmod(hs, SUB)
    return u, h, s, pc, (CH if pc < u else P * (s + 1))


def pieces_of(slot, head_step):
    lo, hi = SLOT_PIECES[slot]
    n, spread = hi - lo, SLOT_SPREAD[slot]
    at = min(head_step, spread)
    return range(lo + n * at // spread, lo + n * min(head_step + 1, spread) // spread)


def tiles_of(u, step):
    if step < 2 * u:
        return [(2 * step, 0, 0), (2 * step + 1, 0, CH)]
    d = 2 * (step - 2 * u)
    first = (SUB * u + d, P * d, 0)
    return [first, (SUB * u + d + 1, P * (d + 1), CH - P * d)]


def build(nc, x, w_in_t, w_r_t, w_k_t, w_v_t, w_out_t, mu_rk, out):
    parts_d = nc.dram_tensor("parts_d", [3, 2 * B, C, T], BF16, kind="Internal").ap()
    vpad_d = nc.dram_tensor("vpad_d", [B * NG, P, NT, GH * HW], F32, kind="Internal").ap()
    ffn_d = nc.dram_tensor("ffn_d", [B * T, C], F32, kind="Internal").ap()

    with ExitStack() as whole:
        ident = whole.enter_context(nc.sbuf_tensor("ident", [P, P], F32))
        ident16 = whole.enter_context(nc.sbuf_tensor("ident16", [P, P], BF16))
        w_out_sb = whole.enter_context(nc.sbuf_tensor("w_out_sb", [P, CC, C], F32))
        consts_ready = whole.enter_context(nc.semaphore("consts_ready"))
        stage_tokens(nc, x, w_in_t, w_r_t, w_k_t, w_v_t, w_out_t, mu_rk,
                     parts_d, vpad_d, ffn_d, ident, ident16, w_out_sb, consts_ready)
        attn_t = whole.enter_context(nc.sbuf_tensor("attn_t", [P, B * CC, T], F32))
        stage_attention(nc, parts_d, vpad_d, ident, ident16, attn_t)
        stage_output(nc, ffn_d, ident, w_out_sb, attn_t, out)


def stage_tokens(nc, x, w_in_t, w_r_t, w_k_t, w_v_t, w_out_t, mu_rk,
                 parts_d, vpad_d, ffn_d, ident, ident16, w_out_sb, consts_ready):
    with ExitStack() as ctx:
        def sb(name, shape, dt=F32):
            return ctx.enter_context(nc.sbuf_tensor(name, shape, dt))

        def ps(name, shape):
            return ctx.enter_context(nc.psum_tensor(name, shape, F32))

        def sem(name):
            return ctx.enter_context(nc.semaphore(name))

        w_in_sb = sb("w_in_sb", [P, CC, 3 * C])
        w_r_sb = sb("w_r_sb", [P, CC, C])
        w_k_sb = sb("w_k_sb", [P, CC, C])
        w_v_sb = sb("w_v_sb", [P, CC, C])
        mu = sb("mu", [P, 2, CC])
        one_less_mu = sb("one_less_mu", [P, 2, CC])
        zeros = sb("zeros", [P, CC, 1])
        x_in = sb("x_in", [P, 2, SUB, C])
        stats = sb("stats", [P, SUB, 6])
        mean_var = sb("mean_var", [P, SUB, 2])
        var_eps = sb("var_eps", [P, SUB])
        root = sb("root", [P, SUB])
        inv_root = sb("inv_root", [P, SUB])
        fix = sb("fix", [P, SUB])
        rstd = sb("rstd", [P, SUB])
        xn = sb("xn", [P, SUB, C])
        xn_t = sb("xn_t", [P, CC, CH + 1])
        mixed = sb("mixed", [P, 2, CC, CH])
        prev_term = sb("prev_term", [P, 2, CC, CH])
        parts = sb("parts", [P, 2, 3, 2 * CC, CH], BF16)
        rest = sb("rest", [P, 2, CH])
        v_pad = sb("v_pad", [P, 2, SUB, H, HW])
        gate = sb("gate", [P, SUB, C])
        relu = sb("relu", [P, CC, CH])
        k_act = sb("k_act", [P, CC, CH])
        ffn = sb("ffn", [P, 2, SUB, C])

        ps_xt = ps("ps_xt", [P, CC, CH])
        ps_qk = ps("ps_qk", [P, 2, CH])
        ps_v = ps("ps_v", [P, SUB, C])
        ps_r = ps("ps_r", [P, SUB, C])

        weights_loaded, mu_loaded = sem("weights_loaded"), sem("mu_loaded")
        x_loaded = [sem("x_loaded0"), sem("x_loaded1")]
        parts_stored = [sem("parts_stored0"), sem("parts_stored1")]
        v_stored = [sem("v_stored0"), sem("v_stored1")]
        ffn_stored = [sem("ffn_stored0"), sem("ffn_stored1")]
        setup_done, mu_ready = sem("setup_done"), sem("mu_ready")
        stats_ready, aggr_ready, var_ready = sem("stats_ready"), sem("aggr_ready"), sem("var_ready")
        root_ready, newton, rstd_ready = sem("root_ready"), sem("newton"), sem("rstd_ready")
        xn_ready, xt_ready, halo_ready, xn_t_ready = sem("xn_ready"), sem("xt_ready"), sem("halo_ready"), sem("xn_t_ready")
        prev_ready, mixed_ready = sem("prev_ready"), sem("mixed_ready")
        qk_ready, hi_ready, rest_ready, mid_ready, parts_ready = (
            sem("qk_ready"), sem("hi_ready"), sem("rest_ready"), sem("mid_ready"), sem("parts_ready"))
        v_ready, v_pad_ready = sem("v_ready"), sem("v_pad_ready")
        r_ready, gate_ready = sem("r_ready"), sem("gate_ready")
        kt_ready, relu_ready, k_act_ready = sem("kt_ready"), sem("relu_ready"), sem("k_act_ready")
        o_ready, gated_ready, ffn_ready = sem("o_ready"), sem("gated_ready"), sem("ffn_ready")

        x_tiles = x.rearrange("(n s p) c -> n p s c", s=SUB, p=P)
        ffn_tiles = ffn_d.rearrange("(n s p) c -> n p s c", s=SUB, p=P)
        by_channel = "(cc p) n -> p cc n"
        passed = sem("passed")
        CREDIT = 16
        block = ctx.enter_context(nc.Block())

        @block.sync
        def _(sp):
            sp.dma_start(x_in[:, 0], x_tiles[0]).then_inc(x_loaded[0], 16)
            sp.dma_start(w_in_sb[:], w_in_t.rearrange(by_channel, p=P)).then_inc(weights_loaded, 16)
            sp.dma_start(mu[:], mu_rk).then_inc(mu_loaded, 16)
            for w, w_sb in ((w_r_t, w_r_sb), (w_k_t, w_k_sb), (w_v_t, w_v_sb), (w_out_t, w_out_sb)):
                sp.dma_start(w_sb[:], w.rearrange(by_channel, p=P)).then_inc(weights_loaded, 16)
            for i in range(2):
                sp.sem_inc(parts_stored[i], CREDIT)
                sp.sem_inc(v_stored[i], CREDIT)
                sp.sem_inc(ffn_stored[i], CREDIT)
            sp.sem_inc(ffn_ready, 1)
            with sp.Fori(0, B) as b:
                for c in range(NCH):
                    par = c % 2
                    nxt = b * NCH + c + 1 if c < NCH - 1 else NCH - b * NCH
                    sp.wait_ge(ffn_ready, b * NCH + c + 1)
                    sp.sem_inc(passed, 1)
                    sp.dma_start(x_in[:, 1 - par], x_tiles[nxt]).then_inc(x_loaded[1 - par], 16)
                    sp.wait_ge(parts_ready, (b * NCH + c + 1) * 4)
                    for part in range(3):
                        dst = parts_d[part].rearrange("(z b) (cc p) t -> b p z cc t", b=B, p=P)
                        for z in range(2):
                            sp.dma_start(dst[b, :, z, :, c * CH:(c + 1) * CH],
                                         parts[:, par, part, z * CC:(z + 1) * CC]).then_inc(parts_stored[par], 16)
                    sp.wait_ge(v_pad_ready, (b * NCH + c + 1) * 2)
                    dst = vpad_d.rearrange("(b g) p t f -> b p t g f", b=B)
                    for s in range(SUB):
                        sp.dma_start(dst[b, :, c * SUB + s],
                                     v_pad[:, par, s].rearrange("p (g h) w -> p g (h w)", h=GH)).then_inc(v_stored[par], 16)
                    sp.wait_ge(ffn_ready, b * NCH + c + 2)
                    sp.dma_start(ffn_tiles[b * NCH + c], ffn[:, par]).then_inc(ffn_stored[par], 16)
            for i in range(2):
                sp.wait_ge(parts_stored[i], CREDIT + NCH * 6 * 16)
                sp.wait_ge(v_stored[i], CREDIT + NCH * SUB * 16)
                sp.wait_ge(ffn_stored[i], CREDIT + NCH * 16)
            sp.wait_ge(x_loaded[0], 16 * (NCH + 1))
            sp.wait_ge(x_loaded[1], 16 * NCH)

        @block.gpsimd
        def _(pool):
            pool.memset(ident[:], 0.0).then_inc(setup_done, 1)
            pool.memset(ident16[:], 0.0).then_inc(setup_done, 1)
            pool.memset(zeros[:], 0.0).then_inc(setup_done, 1)
            pool.memset(v_pad[:, :, :, :, HD:HW], 1.0).then_inc(setup_done, 1)
            pool.wait_ge(setup_done, 4)
            for m in (ident, ident16):
                pool.affine_select(out=m[:], in_=m[:], compare_op=ALU.not_equal, fill=1.0, base=0,
                                   pattern=[[-1, P]], channel_multiplier=1).then_inc(consts_ready, 1)
            with pool.Fori(0, B) as b:
                for c in range(NCH):
                    par = c % 2
                    pool.wait_ge(gated_ready, b * NCH + c + 1)
                    pool.tensor_tensor(ffn[:, par], ffn[:, par], x_in[:, par], ALU.add).then_inc(ffn_ready, 1)

        def token_stats(dve, n, par, loads):
            dve.wait_ge(x_loaded[par], 16 * loads)
            for s in range(SUB):
                dve.bn_stats(stats[:, s], x_in[:, par, s]).then_inc(stats_ready, 1)
            dve.wait_ge(stats_ready, n * SUB + SUB)
            dve.sem_inc(passed, 1)
            for s in range(SUB):
                dve.bn_aggr(mean_var[:, s], stats[:, s]).then_inc(aggr_ready, 1)
            dve.wait_ge(aggr_ready, n * SUB + SUB)
            dve.tensor_scalar(var_eps[:], mean_var[:, :, 1], EPS, None, ALU.add).then_inc(var_ready, 1)

        def normalise_tokens(dve, n, par):
            dve.wait_ge(root_ready, n + 1)
            dve.reciprocal(inv_root[:], root[:]).then_inc(newton, 1)
            dve.wait_ge(newton, n * 4 + 1)
            dve.tensor_tensor(fix[:], inv_root[:], inv_root[:], ALU.mult).then_inc(newton, 1)
            dve.wait_ge(newton, n * 4 + 2)
            dve.tensor_tensor(fix[:], fix[:], var_eps[:], ALU.mult).then_inc(newton, 1)
            dve.wait_ge(newton, n * 4 + 3)
            dve.tensor_scalar(fix[:], fix[:], -0.5, 1.5, ALU.mult, ALU.add).then_inc(newton, 1)
            dve.wait_ge(newton, n * 4 + 4)
            dve.tensor_tensor(rstd[:], inv_root[:], fix[:], ALU.mult).then_inc(rstd_ready, 1)
            dve.wait_ge(rstd_ready, n + 1)
            for s in range(SUB):
                dve.tensor_scalar(xn[:, s], x_in[:, par, s], mean_var[:, s, 0:1], rstd[:, s:s + 1],
                                  ALU.subtract, ALU.mult).then_inc(xn_ready, 1)

        @block.vector
        def _(dve):
            dve.wait_ge(mu_loaded, 16)
            dve.tensor_scalar(one_less_mu[:], mu[:], -1.0, 1.0, ALU.mult, ALU.add).then_inc(mu_ready, 1)
            token_stats(dve, 0, 0, 1)
            normalise_tokens(dve, 0, 0)
            dve.wait_ge(mu_ready, 1)
            with dve.Fori(0, B) as b:
                for c in range(NCH):
                    par = c % 2
                    n = b * NCH + c
                    dve.wait_ge(xn_t_ready, n + 1)
                    for z in range(2):
                        for cc in range(CC):
                            dve.tensor_scalar(prev_term[:, z, cc], xn_t[:, cc, 0:CH], one_less_mu[:, z, cc:cc + 1],
                                              None, ALU.mult).then_inc(prev_ready, 1)
                    for z in range(2):
                        for cc in range(CC):
                            dve.wait_ge(prev_ready, n * 4 + 2 * z + cc + 1)
                            dve.scalar_tensor_tensor(mixed[:, z, cc], xn_t[:, cc, 1:CH + 1], mu[:, z, cc:cc + 1],
                                                     prev_term[:, z, cc], ALU.mult, ALU.add).then_inc(mixed_ready, 1)
                    for j in range(2 * CC):
                        dve.wait_ge(hi_ready, n * 4 + j + 1)
                        dve.scalar_tensor_tensor(rest[:, j % 2], ps_qk[:, j % 2], SCALE if j < CC else 1.0,
                                                 parts[:, par, 0, j], ALU.mult, ALU.subtract).then_inc(rest_ready, 1)
                        dve.wait_ge(rest_ready, n * 4 + j + 1)
                        dve.tensor_copy(parts[:, par, 1, j], rest[:, j % 2]).then_inc(mid_ready, 1)
                        dve.wait_ge(mid_ready, n * 4 + j + 1)
                        dve.tensor_tensor(parts[:, par, 2, j], rest[:, j % 2], parts[:, par, 1, j],
                                          ALU.subtract).then_inc(parts_ready, 1)
                    token_stats(dve, n + 1, 1 - par, b * 2 + (c + 1) // 2 + 1)
                    dve.wait_ge(relu_ready, n + 1)
                    dve.tensor_tensor(k_act[:], relu[:], relu[:], ALU.mult).then_inc(k_act_ready, 1)
                    normalise_tokens(dve, n + 1, 1 - par)
                    dve.wait_ge(o_ready, n + 1)
                    dve.wait_ge(gate_ready, n + 1)
                    dve.wait_ge(ffn_stored[par], CREDIT * (b * 2 + c // 2 + 1))
                    dve.tensor_tensor(ffn[:, par], gate[:],
                                      ps_qk[:].rearrange("p a (s c) -> p (a s) c", c=C), ALU.mult).then_inc(gated_ready, 1)

        @block.scalar
        def _(act):
            def take_root(n):
                act.wait_ge(var_ready, n + 1)
                act.activation(root[:], var_eps[:], ACT.Sqrt).then_inc(root_ready, 1)

            take_root(0)
            act.wait_ge(setup_done, 4)
            with act.Fori(0, B) as b:
                for c in range(NCH):
                    par = c % 2
                    n = b * NCH + c
                    stores = b * 2 + c // 2
                    act.wait_ge(xt_ready, n + 1)
                    act.copy(xn_t[:, :, 0:1], zeros[:] if c == 0 else xn_t[:, :, CH:CH + 1]).then_inc(halo_ready, 1)
                    act.wait_ge(halo_ready, n + 1)
                    act.copy(xn_t[:, :, 1:CH + 1], ps_xt[:]).then_inc(xn_t_ready, 1)
                    act.wait_ge(parts_stored[par], stores * 96 + CREDIT)
                    for j in range(2 * CC):
                        act.wait_ge(qk_ready, n * 4 + j + 1)
                        act.activation(parts[:, par, 0, j], ps_qk[:, j % 2], ACT.Copy,
                                       scale=SCALE if j < CC else 1.0).then_inc(hi_ready, 1)
                    act.wait_ge(v_stored[par], stores * (SUB * 16) + CREDIT)
                    for half in range(2):
                        act.wait_ge(v_ready, n * 2 + half + 1)
                        act.copy(v_pad[:, par, 2 * half:2 * half + 2, :, 0:HD],
                                 ps_v[:, 2 * half:2 * half + 2].rearrange("p s (h d) -> p s h d", d=HD)).then_inc(v_pad_ready, 1)
                    act.wait_ge(r_ready, n + 1)
                    act.activation(gate[:], ps_r[:], ACT.Sigmoid).then_inc(gate_ready, 1)
                    act.wait_ge(kt_ready, n + 1)
                    act.activation(relu[:], ps_xt[:], ACT.Relu).then_inc(relu_ready, 1)
                    take_root(n + 1)

        @block.tensor
        def _(pe):
            pe.wait_ge(consts_ready, 2)
            pe.wait_ge(weights_loaded, 16 * 5)
            with pe.Fori(0, B) as b:
                for c in range(NCH):
                    n = b * NCH + c
                    pe.wait_ge(xn_ready, n * SUB + SUB)
                    for cc in range(CC):
                        for s in range(SUB):
                            last = pe.transpose(ps_xt[:, cc, s * P:(s + 1) * P], xn[:, s, cc * P:(cc + 1) * P], ident[:])
                    last.then_inc(xt_ready, 1)
                    pe.wait_ge(xn_t_ready, n + 1)
                    for j in range(2 * CC):
                        if j >= 2:
                            pe.wait_ge(rest_ready, n * 4 + j - 1)
                        elif c > 0:
                            pe.wait_ge(gated_ready, n)
                        for cc in range(CC):
                            last = pe.matmul(ps_qk[:, j % 2], w_in_sb[:, cc, j * P:(j + 1) * P],
                                             xn_t[:, cc, 1:CH + 1], start=(cc == 0), stop=(cc == CC - 1))
                        last.then_inc(qk_ready, 1)
                    for s in range(SUB):
                        for cc in range(CC):
                            last = pe.matmul(ps_v[:, s], xn_t[:, cc, 1 + s * P:1 + (s + 1) * P],
                                             w_in_sb[:, cc, 2 * C:3 * C], start=(cc == 0), stop=(cc == CC - 1))
                        if s % 2:
                            last.then_inc(v_ready, 1)
                    pe.wait_ge(mixed_ready, n * 4 + 2)
                    for s in range(SUB):
                        for cc in range(CC):
                            last = pe.matmul(ps_r[:, s], mixed[:, 0, cc, s * P:(s + 1) * P], w_r_sb[:, cc],
                                             start=(cc == 0), stop=(cc == CC - 1))
                    last.then_inc(r_ready, 1)
                    pe.wait_ge(mixed_ready, n * 4 + 4)
                    for m in range(CC):
                        for cc in range(CC):
                            last = pe.matmul(ps_xt[:, m], w_k_sb[:, cc, m * P:(m + 1) * P], mixed[:, 1, cc],
                                             start=(cc == 0), stop=(cc == CC - 1))
                    last.then_inc(kt_ready, 1)
                    pe.wait_ge(v_pad_ready, n * 2 + 2)
                    pe.wait_ge(gate_ready, n + 1)
                    pe.wait_ge(parts_ready, n * 4 + 4)
                    pe.wait_ge(k_act_ready, n + 1)
                    for s in range(SUB):
                        for m in range(CC):
                            last = pe.matmul(ps_qk[:, s // 2, (s % 2) * C:(s % 2 + 1) * C],
                                             k_act[:, m, s * P:(s + 1) * P], w_v_sb[:, m],
                                             start=(m == 0), stop=(m == CC - 1))
                    last.then_inc(o_ready, 1)
                pe.wait_ge(gated_ready, b * NCH + NCH)


def stage_attention(nc, parts_d, vpad_d, ident, ident16, attn_t):
    with ExitStack() as ctx:
        def sb(name, shape, dt=F32):
            return ctx.enter_context(nc.sbuf_tensor(name, shape, dt))

        def ps(name, shape):
            return ctx.enter_context(nc.psum_tensor(name, shape, F32))

        def sem(name):
            return ctx.enter_context(nc.semaphore(name))

        q_op = sb("q_op", [P, 2, GH, T], BF16)
        k_op = sb("k_op", [P, 2, GH, T], BF16)
        v_sb = sb("v_sb", [P, 2, NT, GH * HW])
        after = sb("after", [P, NT, GH * HW])
        v_after = sb("v_after", [P, 2, NT, GH * HW])
        keys_after = sb("keys_after", [P, P])
        ones = sb("ones", [P, P])
        mask16 = sb("mask16", [P, P], BF16)
        floor = sb("floor", [P, GH, NT])
        probs = sb("probs", [P, PRING, 2 * CH])
        part_max = sb("part_max", [P, GH * SUB, NCH])
        raw_max = sb("raw_max", [P, GH, SUB])
        row_max = sb("row_max", [P, 4, GH, SUB])
        shift_rest = sb("shift_rest", [P, GH, SUB])
        shift = sb("shift", [P, 4, SUB, 3, GH], BF16)
        shift_t = sb("shift_t", [3 * GH, 2, CH], BF16)
        masked_weight = sb("masked_weight", [P, 4, GH * SUB])
        diag_weight = sb("diag_weight", [P, 2, GH * SUB, P])
        sums = sb("sums", [P, 2, CH])
        turned = sb("turned", [P, CH])
        inv_denom = sb("inv_denom", [P, CH // HW])
        normed = sb("normed", [P, 2, CH])

        ps_s = ps("ps_s", [P, 2, 2 * CH])
        ps_m = ps("ps_m", [P, 2, CH])
        ps_o = ps("ps_o", [P, CH])
        ps_x = ps("ps_x", [P, CH])
        ps_shift = ps_x[:].bitcast(BF16)

        consts_set, consts_made = sem("consts_set"), sem("consts_made")
        q_loaded = [sem("q_loaded0"), sem("q_loaded1")]
        k_loaded = [sem("k_loaded0"), sem("k_loaded1")]
        v_loaded = [sem("v_loaded0"), sem("v_loaded1")]
        piece_ready, piece_reduced = sem("piece_ready"), sem("piece_reduced")
        raw_ready, max_ready, hi_ready, rest_ready, mid_ready, shift_ready = (
            sem("raw_ready"), sem("max_ready"), sem("shift_hi_ready"), sem("shift_rest_ready"),
            sem("shift_mid_ready"), sem("shift_ready"))
        shift_turned, shift_t_ready = sem("shift_turned"), sem("shift_t_ready")
        shift_loaded = [sem("shift_loaded0"), sem("shift_loaded1")]
        weight_ready, diag_ready = sem("weight_ready"), sem("diag_ready")
        after_ready, suffix_ready, v_after_ready = sem("after_ready"), sem("suffix_ready"), sem("v_after_ready")
        scores_ready, probs_ready, probs_masked, probs_used = (
            sem("scores_ready"), sem("probs_ready"), sem("probs_masked"), sem("probs_used"))
        out_ready, sums_ready, denom_ready, normed_ready = (
            sem("out_ready"), sem("sums_ready"), sem("denom_ready"), sem("normed_ready"))
        turned_ready, divided = sem("turned_ready"), sem("divided")
        normed_stored = [sem("normed_stored0"), sem("normed_stored1")]
        passed = sem("passed_mask")
        LOADS = 6 * 16
        CREDIT = 16
        block = ctx.enter_context(nc.Block())

        parts_in = parts_d.rearrange("r (z b) (cc g h d) t -> r z (b cc) g d h t", b=B, cc=CC, g=2, h=GH)
        v_in = vpad_d.rearrange("(i g) p t f -> i g p t f", g=2)

        def unit_of(i, p, u):
            return (i * 2 + p) * NCH + u

        @block.sync
        def _(sp):
            for s in normed_stored:
                sp.sem_inc(s, CREDIT)
            sp.sem_inc(normed_ready, 2)
            for s in shift_loaded:
                sp.sem_inc(s, 48)
            sp.sem_inc(piece_reduced, 2)
            sp.sem_inc(probs_ready, 2)
            sp.sem_inc(probs_used, 2)
            sp.sem_inc(out_ready, 2)
            sp.sem_inc(sums_ready, 1)

            def load_group(i, p):
                for r in range(len(Q_PARTS)):
                    rows = slice(r * HD, (r + 1) * HD)
                    sp.dma_start(q_op[rows, p], parts_in[Q_PARTS[r], 0, i, p]).then_inc(q_loaded[p], 16)
                    sp.dma_start(k_op[rows, p], parts_in[K_PARTS[r], 1, i, p]).then_inc(k_loaded[p], 16)
                sp.dma_start(v_sb[:, p], v_in[i, p]).then_inc(v_loaded[p], 16)

            def place_shift(i, p, u, n):
                sp.wait_ge(shift_t_ready, n + 1)
                for part in range(3):
                    sp.dma_start(q_op[ROWS + part:ROWS + part + 1, p, :, u * CH:(u + 1) * CH],
                                 shift_t[part * GH:(part + 1) * GH, u % 2]).then_inc(shift_loaded[u % 2], 16)

            def keep_normed(i, p, u):
                sp.wait_ge(normed_ready, unit_of(i, p, u) + 3)
                for h in range(GH):
                    row = (p * GH + h) * HD
                    sp.dma_start(attn_t[row:row + HD, i, u * CH:(u + 1) * CH],
                                 normed[h * HW:h * HW + HD, u % 2]).then_inc(normed_stored[u % 2], 16)

            def group(i, p, last):
                if not last:
                    sp.wait_ge(out_ready, unit_of(i, p, 0) + 2)
                    load_group(i + p, 1 - p)
                place_shift(i, p, 2, unit_of(i, p, 2))
                keep_normed(i, p, 0)
                place_shift(i, p, 3, unit_of(i, p, 3))
                keep_normed(i, p, 1)
                if not last:
                    place_shift(i, 1 - p, 0, unit_of(i, p, 4))
                keep_normed(i, p, 2)
                if not last:
                    place_shift(i, 1 - p, 1, unit_of(i, p, 5))
                keep_normed(i, p, 3)

            load_group(0, 0)
            place_shift(0, 0, 0, 0)
            place_shift(0, 0, 1, 1)
            with sp.Fori(0, B * CC - 1) as i:
                group(i, 0, False)
                group(i, 1, False)
            group(B * CC - 1, 0, False)
            group(B * CC - 1, 1, True)
            for s in normed_stored:
                sp.wait_ge(s, CREDIT + B * NG * NCH // 2 * GH * 16)

        def add_up_after(pool, p, n, loads):
            pool.wait_ge(v_loaded[p], 16 * loads)
            for j in range(NT - 2, -1, -1):
                k = NT - 2 - j
                if j < NT - 2:
                    pool.wait_ge(after_ready, n * (NT - 1) + k)
                pool.tensor_tensor(after[:, j], after[:, j + 1], v_sb[:, p, j + 1], ALU.add).then_inc(after_ready, 1)

        @block.gpsimd
        def _(pool):
            pool.memset(ones[:], 1.0).then_inc(consts_set, 1)
            pool.memset(mask16[:], 0.0).then_inc(consts_set, 1)
            pool.memset(floor[:], 0.0).then_inc(consts_set, 1)
            pool.memset(after[:, NT - 1], 0.0).then_inc(consts_set, 1)
            pool.wait_ge(consts_set, 4)
            pool.memset(k_op[ROWS:KROWS], 1.0).then_inc(consts_set, 1)
            pool.wait_ge(consts_set, 5)
            pool.affine_select(out=keys_after[:], in_=ones[:], compare_op=ALU.is_gt, fill=0.0, base=0,
                               pattern=[[-1, P]], channel_multiplier=1).then_inc(consts_made, 1)
            pool.affine_select(out=mask16[:], in_=mask16[:], compare_op=ALU.is_ge, fill=NEG, base=0,
                               pattern=[[-1, P]], channel_multiplier=1).then_inc(consts_made, 1)
            pool.affine_select(out=floor[:, :, NT - 1], in_=floor[:, :, NT - 1], compare_op=ALU.not_equal, fill=LOWEST,
                               base=-(P - 1), pattern=[[0, GH]], channel_multiplier=1).then_inc(consts_made, 1)

            def group(i, p, last):
                for u in range(NCH):
                    for step in (2 * u, 2 * u + 1):
                        for h in range(GH):
                            slot = (STEP0[u] + step) * GH + h
                            pool.wait_ge(probs_ready, (i * 2 + p) * (GSTEPS * GH) + slot + 3)
                            pool.sem_inc(passed, 1)
                            for _, _, col in tiles_of(u, step):
                                blk = probs[:, slot % PRING, col:col + P]
                                done = pool.affine_select(out=blk, in_=blk, compare_op=ALU.is_ge, fill=0.0, base=0,
                                                          pattern=[[1, P]], channel_multiplier=-1)
                            done.then_inc(probs_masked, 1)
                        if step == 2 * u:
                            n = unit_of(i, p, u)
                            pool.wait_ge(weight_ready, n + 1)
                            pool.wait_ge(out_ready, n + 1)
                            pool.tensor_tensor(diag_weight[:, u % 2], ident[:].unsqueeze(1).broadcast_to([P, GH * SUB, P]),
                                               masked_weight[:, u].unsqueeze(2).broadcast_to([P, GH * SUB, P]),
                                               ALU.mult).then_inc(diag_ready, 1)
                    if u == NCH - 2 and not last:
                        pool.wait_ge(v_after_ready, (i * 2 + p) * 4 + 4)
                        add_up_after(pool, 1 - p, i * 2 + p + 1, i + 1 + p)

            add_up_after(pool, 0, 0, 1)
            with pool.Fori(0, B * CC - 1) as i:
                group(i, 0, False)
                group(i, 1, False)
            group(B * CC - 1, 0, False)
            group(B * CC - 1, 1, True)

        @block.scalar
        def _(act):
            def weight(n, u):
                act.wait_ge(max_ready, n + 1)
                act.activation(masked_weight[:, u], row_max[:, u].rearrange("p h s -> p (h s)"), ACT.Exp,
                               scale=-1.0).then_inc(weight_ready, 1)

            def keep_suffix(p, quad, n):
                act.wait_ge(suffix_ready, n + 1)
                act.copy(v_after[:, p, quad * SUB:(quad + 1) * SUB],
                         ps_x[:].rearrange("p (s f) -> p s f", s=SUB)).then_inc(v_after_ready, 1)

            def group(i, p, last):
                for u in range(NCH):
                    for step in range(STEPS[u]):
                        width = sum(CH - q0 for _, q0, _ in tiles_of(u, step))
                        t = STEP0[u] + step
                        act.wait_ge(probs_used, (i * 2 + p) * GSTEPS + t + 1)
                        for h in range(GH):
                            slot = t * GH + h
                            act.wait_ge(scores_ready, (i * 2 + p) * (GSTEPS * GH) + slot + 1)
                            act.activation(probs[:, slot % PRING, 0:width], ps_s[:, slot % 2, 0:width],
                                           ACT.Exp).then_inc(probs_ready, 1)
                        if step == 0:
                            if u > 0:
                                keep_sums(unit_of(i, p, u - 1), (u - 1) % 2)
                        if (u, step) in SV_AT and not last:
                            keep_suffix(1 - p, SV_AT[u, step], (i * 2 + p + 1) * 4 + SV_AT[u, step])
                        if (u, step) in SHIFT_AT and not (u == 3 and last):
                            v = SHIFT_AT[u, step]
                            weight(unit_of(i, p, v + (4 if u == 3 else 0)), v)
                keep_sums(unit_of(i, p, NCH - 1), 1)

            def keep_sums(n, par):
                act.wait_ge(out_ready, n + 3)
                act.wait_ge(normed_ready, n + 1)
                act.copy(sums[:, par], ps_o[:]).then_inc(sums_ready, 1)

            for quad in range(4):
                keep_suffix(0, quad, quad)
            weight(0, 0)
            weight(1, 1)
            with act.Fori(0, B * CC - 1) as i:
                group(i, 0, False)
                group(i, 1, False)
            group(B * CC - 1, 0, False)
            group(B * CC - 1, 1, True)

        @block.vector
        def _(dve):
            dve.wait_ge(consts_made, 3)

            def reduce_piece(f, base):
                u, h, s, pc, width = piece(f)
                dve.wait_ge(piece_ready, base + f + 1)
                dve.tensor_reduce(part_max[:, h * SUB + s, pc:pc + 1], ps_m[:, f % 2, 0:width], AX_X,
                                  ALU.max).then_inc(piece_reduced, 1)
                if f + 1 in PIECE0:
                    finish_max(u, base + f + 1)

            def finish_max(u, reduced):
                n = unit_now[0]
                dve.wait_ge(piece_reduced, reduced + 2)
                dve.tensor_reduce(raw_max[:].rearrange("p h s -> p (h s)"), part_max[:, :, 0:u + 1], AX_X,
                                  ALU.max).then_inc(raw_ready, 1)
                dve.wait_ge(raw_ready, n + 1)
                dve.tensor_tensor(row_max[:, u], raw_max[:], floor[:, :, u * SUB:(u + 1) * SUB], ALU.max).then_inc(max_ready, 1)
                dve.wait_ge(max_ready, n + 1)
                by_head = [shift[:, u, :, part].rearrange("p s h -> p h s") for part in range(3)]
                dve.tensor_scalar(by_head[0], row_max[:, u], -1.0, None, ALU.mult).then_inc(hi_ready, 1)
                dve.wait_ge(hi_ready, n + 1)
                dve.scalar_tensor_tensor(shift_rest[:], row_max[:, u], -1.0, by_head[0], ALU.mult,
                                         ALU.subtract).then_inc(rest_ready, 1)
                dve.wait_ge(rest_ready, n + 1)
                dve.tensor_copy(by_head[1], shift_rest[:]).then_inc(mid_ready, 1)
                dve.wait_ge(mid_ready, n + 1)
                dve.tensor_tensor(by_head[2], shift_rest[:], by_head[1], ALU.subtract).then_inc(shift_ready, 1)

            def keep_shift(u, n, earlier):
                dve.wait_ge(shift_turned, n + 1)
                dve.wait_ge(shift_loaded[u % 2], earlier * 48 + 48)
                dve.tensor_copy(shift_t[:, u % 2], ps_shift[0:3 * GH, 0:CH]).then_inc(shift_t_ready, 1)

            def normalise(n, par):
                blocks = turned[:].rearrange("p (b w) -> p b w", w=HW)
                dve.wait_ge(normed_ready, n + 2)
                dve.wait_ge(sums_ready, n + 2)
                dve.transpose(turned[:], sums[:, par]).then_inc(turned_ready, 1)
                dve.wait_ge(turned_ready, n + 1)
                dve.reciprocal(inv_denom[:], blocks[:, :, HD]).then_inc(denom_ready, 1)
                dve.wait_ge(denom_ready, n + 1)
                dve.tensor_tensor(blocks[:, :, 0:HD], blocks[:, :, 0:HD],
                                  inv_denom[:].unsqueeze(2).broadcast_to([P, CH // HW, HD]), ALU.mult).then_inc(divided, 1)
                dve.wait_ge(divided, n + 1)
                dve.wait_ge(normed_stored[par], n_stored[0])
                dve.transpose(normed[:, par], turned[:]).then_inc(normed_ready, 1)

            unit_now, n_stored = [0], [0]

            def group(i, p, last):
                G = i * 2 + p
                for u in range(NCH):
                    ahead = u == NCH - 1
                    for step in range(STEPS[u]):
                        if not (ahead and last):
                            for h in range(GH):
                                for f in pieces_of(u, step * GH + h):
                                    unit_now[0] = unit_of(i, p, piece(f)[0] + (NCH if ahead else 0))
                                    reduce_piece(f, (G + 1 if ahead else G) * PIECES)
                            if (u, step) in SHIFT_AT:
                                v = SHIFT_AT[u, step]
                                keep_shift(v, unit_of(i, p, v + (NCH if ahead else 0)),
                                           (G + 1 if ahead else G) * (NCH // 2) + v // 2)
                        if step == 1 and u > 0:
                            n_stored[0] = (G * (NCH // 2) + (u - 1) // 2) * (GH * 16) + CREDIT
                            normalise(unit_of(i, p, u - 1), (u - 1) % 2)
                n_stored[0] = (G * (NCH // 2) + 1) * (GH * 16) + CREDIT
                normalise(unit_of(i, p, NCH - 1), 1)

            for f in range(HEAD_START):
                unit_now[0] = piece(f)[0]
                reduce_piece(f, 0)
                if f + 1 == PIECE0[1]:
                    keep_shift(0, 0, 0)
                if f + 1 == PIECE0[2]:
                    keep_shift(1, 1, 0)
            with dve.Fori(0, B * CC - 1) as i:
                group(i, 0, False)
                group(i, 1, False)
            group(B * CC - 1, 0, False)
            group(B * CC - 1, 1, True)

        @block.tensor
        def _(pe):
            pe.wait_ge(consts_made, 3)

            def score_piece(f, p, base):
                u, h, s, pc, width = piece(f)
                pe.wait_ge(piece_reduced, base + f + 1)
                q0 = u * CH + s * P
                last = pe.matmul(ps_m[:, f % 2, 0:width], q_op[0:ROWS, p, h, q0:q0 + P],
                                 k_op[0:ROWS, p, h, pc * CH:pc * CH + width], start=True, stop=(pc < u))
                if pc == u:
                    last = pe.matmul(ps_m[:, f % 2, s * P:width], ident16[:], mask16[:], start=False, stop=True)
                last.then_inc(piece_ready, 1)

            def turn_shift(u, n, quads):
                pe.wait_ge(shift_ready, n + 1)
                if not isinstance(n, int) or n > 0:
                    pe.wait_ge(shift_t_ready, n)
                pe.wait_ge(v_after_ready, quads)
                for s in range(SUB):
                    last = pe.transpose(ps_shift[0:3 * GH, s * P:(s + 1) * P],
                                        shift[:, u, s].rearrange("p r h -> p (r h)"), ident16[:])
                last.then_inc(shift_turned, 1)

            def sum_suffix(p, quad, group_n, turned):
                pe.wait_ge(after_ready, (group_n + 1) * (NT - 1))
                if not isinstance(group_n, int) or group_n * 4 + quad > 0:
                    pe.wait_ge(v_after_ready, group_n * 4 + quad)
                if not isinstance(turned, int) or turned > 0:
                    pe.wait_ge(shift_t_ready, turned)
                tiles = slice(quad * SUB, (quad + 1) * SUB)
                pe.matmul(ps_x[:], keys_after[:], v_sb[:, p, tiles].rearrange("p s f -> p (s f)"), start=True, stop=False)
                pe.matmul(ps_x[:], ones[:], after[:, tiles].rearrange("p s f -> p (s f)"),
                          start=False, stop=True).then_inc(suffix_ready, 1)

            def score_step(p, u, step, h, G):
                slot = (STEP0[u] + step) * GH + h
                pe.wait_ge(probs_ready, G * (GSTEPS * GH) + slot + 1)
                for kt, q0, col in tiles_of(u, step):
                    last = pe.matmul(ps_s[:, slot % 2, col:col + CH - q0], k_op[0:KROWS, p, h, kt * P:(kt + 1) * P],
                                     q_op[0:KROWS, p, h, u * CH + q0:(u + 1) * CH], start=True, stop=True)
                last.then_inc(scores_ready, 1)

            def values_step(p, u, step, G, n):
                t = STEP0[u] + step
                if step == 0:
                    pe.wait_ge(sums_ready, n + 1)
                if step < 2 * u:
                    pe.wait_ge(probs_ready, G * (GSTEPS * GH) + (t + 1) * GH + 2)
                else:
                    pe.wait_ge(probs_masked, n * (2 * GH) + (step - 2 * u + 1) * GH)
                for kt, q0, col in tiles_of(u, step):
                    for h in range(GH):
                        last = pe.matmul(ps_o[h * HW:(h + 1) * HW, q0:CH], v_sb[:, p, kt, h * HW:(h + 1) * HW],
                                         probs[:, (t * GH + h) % PRING, col:col + CH - q0],
                                         start=(kt == 0), stop=False)
                last.then_inc(probs_used, 1)

            def masked_keys(p, u, G, n):
                pe.wait_ge(diag_ready, n + 1)
                pe.wait_ge(v_after_ready, G * 4 + 4)
                for s in range(SUB):
                    for h in range(GH):
                        last = pe.matmul(ps_o[h * HW:(h + 1) * HW, s * P:(s + 1) * P],
                                         v_after[:, p, u * SUB + s, h * HW:(h + 1) * HW],
                                         diag_weight[:, u % 2, h * SUB + s], start=False, stop=(s == SUB - 1))
                last.then_inc(out_ready, 1)

            def group(i, p, last_group):
                G = i * 2 + p
                for u in range(NCH):
                    ahead = u == NCH - 1
                    if u == 0:
                        pe.wait_ge(q_loaded[p], (i + 1) * LOADS)
                        pe.wait_ge(k_loaded[p], (i + 1) * LOADS)
                    pe.wait_ge(shift_loaded[u % 2], (G * (NCH // 2) + u // 2 + 2) * 48)
                    if ahead and not last_group:
                        pe.wait_ge(q_loaded[1 - p], (i + 1 + p) * LOADS)
                        pe.wait_ge(k_loaded[1 - p], (i + 1 + p) * LOADS)
                    for step in range(STEPS[u]):
                        for h in range(GH):
                            score_step(p, u, step, h, G)
                            if not (ahead and last_group):
                                for f in pieces_of(u, step * GH + h):
                                    score_piece(f, 1 - p if ahead else p, (G + 1 if ahead else G) * PIECES)
                        if step > 0:
                            values_step(p, u, step - 1, G, unit_of(i, p, u))
                        if (u, step) in SV_AT and not last_group:
                            sum_suffix(1 - p, SV_AT[u, step], G + 1, unit_of(i, p, 4 + (step > 3)))
                        if (u, step) in SHIFT_AT and not (ahead and last_group):
                            v = SHIFT_AT[u, step]
                            quads = (G + 1) * 4 + (sum(s < step for _, s in SV_AT) if ahead else 0)
                            turn_shift(v, unit_of(i, p, v + (NCH if ahead else 0)), quads)
                    values_step(p, u, STEPS[u] - 1, G, unit_of(i, p, u))
                    masked_keys(p, u, G, unit_of(i, p, u))

            pe.wait_ge(q_loaded[0], LOADS)
            pe.wait_ge(k_loaded[0], LOADS)
            pe.wait_ge(v_loaded[0], 16)
            for quad in range(4):
                sum_suffix(0, quad, 0, 0)
            for f in range(HEAD_START):
                score_piece(f, 0, 0)
                if f + 1 == PIECE0[1]:
                    turn_shift(0, 0, 4)
                if f + 1 == PIECE0[2]:
                    turn_shift(1, 1, 4)
            with pe.Fori(0, B * CC - 1) as i:
                group(i, 0, False)
                group(i, 1, False)
            group(B * CC - 1, 0, False)
            group(B * CC - 1, 1, True)


def stage_output(nc, ffn_d, ident, w_out_sb, attn_t, out):
    with ExitStack() as ctx:
        def sb(name, shape, dt=F32):
            return ctx.enter_context(nc.sbuf_tensor(name, shape, dt))

        def sem(name):
            return ctx.enter_context(nc.semaphore(name))

        ffn = sb("ffn_in", [P, 2, SUB, C])
        attn = sb("attn_chunk", [P, 2, CC, CH])
        total = sb("total", [P, 2, SUB, C])
        ps_y = ctx.enter_context(nc.psum_tensor("ps_y", [P, 2, SUB, C], F32))
        ffn_loaded = [sem("ffn_loaded0"), sem("ffn_loaded1")]
        out_stored = [sem("out_stored0"), sem("out_stored1")]
        attn_ready, y_ready, total_ready = sem("attn_ready"), sem("y_ready"), sem("total_ready")
        ffn_tiles = ffn_d.rearrange("(n s p) c -> n p s c", s=SUB, p=P)
        out_tiles = out.rearrange("(n s p) c -> n p s c", s=SUB, p=P)
        block = ctx.enter_context(nc.Block())

        @block.sync
        def _(sp):
            sp.sem_inc(y_ready, 2)
            sp.sem_inc(total_ready, 2)
            sp.sem_inc(out_stored[0], 16)
            sp.sem_inc(out_stored[1], 16)
            with sp.Fori(0, B) as b:
                for c in range(NCH):
                    sp.wait_ge(total_ready, b * NCH + c + 3)
                    sp.dma_start(out_tiles[b * NCH + c], total[:, c % 2]).then_inc(out_stored[c % 2], 16)
            for s in out_stored:
                sp.wait_ge(s, 16 + B * 2 * 16)

        @block.scalar
        def _(act):
            with act.Fori(0, B) as b:
                for c in range(NCH):
                    act.wait_ge(y_ready, b * NCH + c + 1)
                    act.copy(attn[:, c % 2], attn_t[:, bass.ds(b * CC, CC), c * CH:(c + 1) * CH]).then_inc(attn_ready, 1)

        @block.tensor
        def _(pe):
            with pe.Fori(0, B) as b:
                for c in range(NCH):
                    pe.wait_ge(attn_ready, b * NCH + c + 1)
                    pe.wait_ge(total_ready, b * NCH + c + 1)
                    for s in range(SUB):
                        for cc in range(CC):
                            last = pe.matmul(ps_y[:, c % 2, s], attn[:, c % 2, cc, s * P:(s + 1) * P],
                                             w_out_sb[:, cc], start=(cc == 0), stop=(cc == CC - 1))
                    last.then_inc(y_ready, 1)

        @block.vector
        def _(dve):
            with dve.Fori(0, B) as b:
                for c in range(NCH):
                    dve.wait_ge(ffn_loaded[c % 2], (b * 2 + c // 2 + 1) * 16)
                    dve.wait_ge(y_ready, b * NCH + c + 3)
                    dve.wait_ge(out_stored[c % 2], (b * 2 + c // 2) * 16 + 16)
                    dve.tensor_tensor(total[:, c % 2], ffn[:, c % 2], ps_y[:, c % 2], ALU.add).then_inc(total_ready, 1)

        @block.gpsimd
        def _(pool):
            with pool.Fori(0, B) as b:
                for c in range(NCH):
                    pool.wait_ge(total_ready, b * NCH + c + 1)
                    pool.dma_start(ffn[:, c % 2], ffn_tiles[b * NCH + c]).then_inc(ffn_loaded[c % 2], 16)


def kernel(L0_attn_x, L0_attn_w_in, L0_attn_w_out, L0_ffn_W_r, L0_ffn_W_k, L0_ffn_W_v, L0_ffn_mu_r, L0_ffn_mu_k):
    import numpy as np
    import concourse.bacc as bacc
    from concourse.bass_utils import run_bass_kernel_spmd

    def laid(a, turn=False):
        a = np.asarray(a)
        return np.ascontiguousarray(a.T if turn else a)

    inputs = {
        "x": laid(L0_attn_x).reshape(B * T, C),
        "w_in_t": laid(L0_attn_w_in, True),
        "w_r_t": laid(L0_ffn_W_r, True),
        "w_k_t": laid(L0_ffn_W_k, True),
        "w_v_t": laid(L0_ffn_W_v, True),
        "w_out_t": laid(L0_attn_w_out, True),
        "mu_rk": laid(np.stack([np.asarray(L0_ffn_mu_r), np.asarray(L0_ffn_mu_k)]).reshape(2, CC, P).transpose(2, 0, 1)),
    }
    nc = bacc.Bacc("TRN2", target_bir_lowering=False, num_devices=1)
    args = [nc.dram_tensor(name, a.shape, F32, kind="ExternalInput").ap() for name, a in inputs.items()]
    y = nc.dram_tensor("y", (B * T, C), F32, kind="ExternalOutput").ap()
    build(nc, *args, y)
    r = run_bass_kernel_spmd(nc, [inputs], core_ids=[0])
    return r.results[0]["y"].reshape(B, T, C)
```

```python
from contextlib import ExitStack

import concourse.bass as bass
from concourse import mybir

F32 = mybir.dt.float32
BF16 = mybir.dt.bfloat16
ALU = mybir.AluOpType
ACT = mybir.ActivationFunctionType
AX_X = mybir.AxisListType.X

P = 128
B, T, C = 2, 2048, 256
H, HD = 16, 16
SCALE = 0.25
EPS = 1e-5
CC = C // P
CH = 512
NCH = T // CH
SUB = CH // P
NT = T // P
GH = 4
NG = H // GH
HW = 32
NEG = -1e30
LOWEST = -3e38

Q_PARTS = (0, 1, 2, 0, 1, 0)
K_PARTS = (0, 0, 0, 1, 1, 2)
ROWS = HD * len(Q_PARTS)
KROWS = ROWS + 3

PIECE0 = [SUB * GH * u * (u + 1) // 2 for u in range(NCH + 1)]
PIECES = PIECE0[NCH]
HEAD_START = PIECE0[2] + 32
SLOT_PIECES = {0: (HEAD_START, PIECE0[3]), 1: (PIECE0[3], PIECE0[3] + 24),
               2: (PIECE0[3] + 24, PIECES), 3: (0, HEAD_START)}
SLOT_SPREAD = {0: 16, 1: 32, 2: 40, 3: 64}
SHIFT_AT = {(3, 5): 0, (3, 11): 1, (1, 2): 2, (2, 10): 3}
SV_AT = {(3, 2): 0, (3, 4): 1, (3, 7): 2, (3, 9): 3}
MAX_STEPS = 6
NORM_STEPS = 4
NORM_AT = 8
KT0 = [SUB * u * (u + 1) // 2 for u in range(NCH + 1)]
KTILES = KT0[NCH]
SLOTS = KTILES * GH
PRING = 16
SRING = 2
MRING = 4


def piece(f):
    u = max(v for v in range(NCH) if PIECE0[v] <= f)
    hs, pc = divmod(f - PIECE0[u], u + 1)
    h, s = divmod(hs, SUB)
    return u, h, s, pc, (CH if pc < u else P * (s + 1))


def pieces_of(slot, head_step):
    lo, hi = SLOT_PIECES[slot]
    n, spread = hi - lo, SLOT_SPREAD[slot]
    at = min(head_step, spread)
    return range(lo + n * at // spread, lo + n * min(at + 1, spread) // spread)


def key_tiles(u):
    return SUB * (u + 1)


def first_query(u, kt):
    return P * max(0, kt - SUB * u)


def build(nc, x, w_in_t, w_r_t, w_k_t, w_v_t, w_out_t, mu_rk, out):
    parts_d = nc.dram_tensor("parts_d", [3, 2 * B, C, T], BF16, kind="Internal").ap()
    vpad_d = nc.dram_tensor("vpad_d", [B * NG, P, NT, GH * HW], F32, kind="Internal").ap()
    ffn_d = nc.dram_tensor("ffn_d", [B * T, C], F32, kind="Internal").ap()

    with ExitStack() as whole:
        ident = whole.enter_context(nc.sbuf_tensor("ident", [P, P], F32))
        ident16 = whole.enter_context(nc.sbuf_tensor("ident16", [P, P], BF16))
        w_out_sb = whole.enter_context(nc.sbuf_tensor("w_out_sb", [P, CC, C], F32))
        consts_ready = whole.enter_context(nc.semaphore("consts_ready"))
        stage_tokens(nc, x, w_in_t, w_r_t, w_k_t, w_v_t, w_out_t, mu_rk,
                     parts_d, vpad_d, ffn_d, ident, ident16, w_out_sb, consts_ready)
        attn_t = whole.enter_context(nc.sbuf_tensor("attn_t", [P, B * CC, T], F32))
        stage_attention(nc, parts_d, vpad_d, ident, ident16, attn_t)
        stage_output(nc, ffn_d, ident, w_out_sb, attn_t, out)


def stage_tokens(nc, x, w_in_t, w_r_t, w_k_t, w_v_t, w_out_t, mu_rk,
                 parts_d, vpad_d, ffn_d, ident, ident16, w_out_sb, consts_ready):
    with ExitStack() as ctx:
        def sb(name, shape, dt=F32):
            return ctx.enter_context(nc.sbuf_tensor(name, shape, dt))

        def ps(name, shape):
            return ctx.enter_context(nc.psum_tensor(name, shape, F32))

        def sem(name):
            return ctx.enter_context(nc.semaphore(name))

        w_in_sb = sb("w_in_sb", [P, CC, 3 * C])
        w_r_sb = sb("w_r_sb", [P, CC, C])
        w_k_sb = sb("w_k_sb", [P, CC, C])
        w_v_sb = sb("w_v_sb", [P, CC, C])
        mu = sb("mu", [P, 2, CC])
        one_less_mu = sb("one_less_mu", [P, 2, CC])
        zeros = sb("zeros", [P, CC, 1])
        x_in = sb("x_in", [P, 2, SUB, C])
        stats = sb("stats", [P, SUB, 6])
        mean_var = sb("mean_var", [P, SUB, 2])
        var_eps = sb("var_eps", [P, SUB])
        root = sb("root", [P, SUB])
        inv_root = sb("inv_root", [P, SUB])
        fix = sb("fix", [P, SUB])
        rstd = sb("rstd", [P, SUB])
        xn = sb("xn", [P, SUB, C])
        xn_t = sb("xn_t", [P, CC, CH + 1])
        mixed = sb("mixed", [P, 2, CC, CH])
        prev_term = sb("prev_term", [P, 2, CC, CH])
        parts = sb("parts", [P, 2, 3, 2 * CC, CH], BF16)
        rest = sb("rest", [P, 2, CH])
        v_pad = sb("v_pad", [P, 2, SUB, H, HW])
        gate = sb("gate", [P, SUB, C])
        relu = sb("relu", [P, CC, CH])
        k_act = sb("k_act", [P, CC, CH])
        ffn = sb("ffn", [P, 2, SUB, C])

        ps_xt = ps("ps_xt", [P, CC, CH])
        ps_qk = ps("ps_qk", [P, 2, CH])
        ps_v = ps("ps_v", [P, SUB, C])
        ps_r = ps("ps_r", [P, SUB, C])

        weights_loaded, mu_loaded = sem("weights_loaded"), sem("mu_loaded")
        x_loaded = [sem("x_loaded0"), sem("x_loaded1")]
        parts_stored = [sem("parts_stored0"), sem("parts_stored1")]
        v_stored = [sem("v_stored0"), sem("v_stored1")]
        ffn_stored = [sem("ffn_stored0"), sem("ffn_stored1")]
        setup_done, mu_ready = sem("setup_done"), sem("mu_ready")
        stats_ready, aggr_ready, var_ready = sem("stats_ready"), sem("aggr_ready"), sem("var_ready")
        root_ready, newton, rstd_ready = sem("root_ready"), sem("newton"), sem("rstd_ready")
        xn_ready, xt_ready, halo_ready, xn_t_ready = sem("xn_ready"), sem("xt_ready"), sem("halo_ready"), sem("xn_t_ready")
        prev_ready, mixed_ready = sem("prev_ready"), sem("mixed_ready")
        qk_ready, hi_ready, rest_ready, mid_ready, parts_ready = (
            sem("qk_ready"), sem("hi_ready"), sem("rest_ready"), sem("mid_ready"), sem("parts_ready"))
        v_ready, v_pad_ready = sem("v_ready"), sem("v_pad_ready")
        r_ready, gate_ready = sem("r_ready"), sem("gate_ready")
        kt_ready, relu_ready, k_act_ready = sem("kt_ready"), sem("relu_ready"), sem("k_act_ready")
        o_ready, gated_ready, ffn_ready = sem("o_ready"), sem("gated_ready"), sem("ffn_ready")

        x_tiles = x.rearrange("(n s p) c -> n p s c", s=SUB, p=P)
        ffn_tiles = ffn_d.rearrange("(n s p) c -> n p s c", s=SUB, p=P)
        by_channel = "(cc p) n -> p cc n"
        passed = sem("passed")
        CREDIT = 16
        block = ctx.enter_context(nc.Block())

        @block.sync
        def _(sp):
            sp.dma_start(x_in[:, 0], x_tiles[0]).then_inc(x_loaded[0], 16)
            sp.dma_start(w_in_sb[:], w_in_t.rearrange(by_channel, p=P)).then_inc(weights_loaded, 16)
            sp.dma_start(mu[:], mu_rk).then_inc(mu_loaded, 16)
            for w, w_sb in ((w_r_t, w_r_sb), (w_k_t, w_k_sb), (w_v_t, w_v_sb), (w_out_t, w_out_sb)):
                sp.dma_start(w_sb[:], w.rearrange(by_channel, p=P)).then_inc(weights_loaded, 16)
            for i in range(2):
                sp.sem_inc(parts_stored[i], CREDIT)
                sp.sem_inc(v_stored[i], CREDIT)
                sp.sem_inc(ffn_stored[i], CREDIT)
            sp.sem_inc(ffn_ready, 1)
            with sp.Fori(0, B) as b:
                for c in range(NCH):
                    par = c % 2
                    nxt = b * NCH + c + 1 if c < NCH - 1 else NCH - b * NCH
                    sp.wait_ge(ffn_ready, b * NCH + c + 1)
                    sp.sem_inc(passed, 1)
                    sp.dma_start(x_in[:, 1 - par], x_tiles[nxt]).then_inc(x_loaded[1 - par], 16)
                    sp.wait_ge(parts_ready, (b * NCH + c + 1) * 4)
                    for part in range(3):
                        dst = parts_d[part].rearrange("(z b) (cc p) t -> b p z cc t", b=B, p=P)
                        for z in range(2):
                            sp.dma_start(dst[b, :, z, :, c * CH:(c + 1) * CH],
                                         parts[:, par, part, z * CC:(z + 1) * CC]).then_inc(parts_stored[par], 16)
                    sp.wait_ge(v_pad_ready, (b * NCH + c + 1) * 2)
                    dst = vpad_d.rearrange("(b g) p t f -> b p t g f", b=B)
                    for s in range(SUB):
                        sp.dma_start(dst[b, :, c * SUB + s],
                                     v_pad[:, par, s].rearrange("p (g h) w -> p g (h w)", h=GH)).then_inc(v_stored[par], 16)
                    sp.wait_ge(ffn_ready, b * NCH + c + 2)
                    sp.dma_start(ffn_tiles[b * NCH + c], ffn[:, par]).then_inc(ffn_stored[par], 16)
            for i in range(2):
                sp.wait_ge(parts_stored[i], CREDIT + NCH * 6 * 16)
                sp.wait_ge(v_stored[i], CREDIT + NCH * SUB * 16)
                sp.wait_ge(ffn_stored[i], CREDIT + NCH * 16)
            sp.wait_ge(x_loaded[0], 16 * (NCH + 1))
            sp.wait_ge(x_loaded[1], 16 * NCH)

        @block.gpsimd
        def _(pool):
            pool.memset(ident[:], 0.0).then_inc(setup_done, 1)
            pool.memset(ident16[:], 0.0).then_inc(setup_done, 1)
            pool.memset(zeros[:], 0.0).then_inc(setup_done, 1)
            pool.memset(v_pad[:, :, :, :, HD:HW], 1.0).then_inc(setup_done, 1)
            pool.wait_ge(setup_done, 4)
            for m in (ident, ident16):
                pool.affine_select(out=m[:], in_=m[:], compare_op=ALU.not_equal, fill=1.0, base=0,
                                   pattern=[[-1, P]], channel_multiplier=1).then_inc(consts_ready, 1)
            with pool.Fori(0, B) as b:
                for c in range(NCH):
                    par = c % 2
                    pool.wait_ge(gated_ready, b * NCH + c + 1)
                    pool.tensor_tensor(ffn[:, par], ffn[:, par], x_in[:, par], ALU.add).then_inc(ffn_ready, 1)

        def token_stats(dve, n, par, loads):
            dve.wait_ge(x_loaded[par], 16 * loads)
            for s in range(SUB):
                dve.bn_stats(stats[:, s], x_in[:, par, s]).then_inc(stats_ready, 1)
            dve.wait_ge(stats_ready, n * SUB + SUB)
            dve.sem_inc(passed, 1)
            for s in range(SUB):
                dve.bn_aggr(mean_var[:, s], stats[:, s]).then_inc(aggr_ready, 1)
            dve.wait_ge(aggr_ready, n * SUB + SUB)
            dve.tensor_scalar(var_eps[:], mean_var[:, :, 1], EPS, None, ALU.add).then_inc(var_ready, 1)

        def normalise_tokens(dve, n, par):
            dve.wait_ge(root_ready, n + 1)
            dve.reciprocal(inv_root[:], root[:]).then_inc(newton, 1)
            dve.wait_ge(newton, n * 4 + 1)
            dve.tensor_tensor(fix[:], inv_root[:], inv_root[:], ALU.mult).then_inc(newton, 1)
            dve.wait_ge(newton, n * 4 + 2)
            dve.tensor_tensor(fix[:], fix[:], var_eps[:], ALU.mult).then_inc(newton, 1)
            dve.wait_ge(newton, n * 4 + 3)
            dve.tensor_scalar(fix[:], fix[:], -0.5, 1.5, ALU.mult, ALU.add).then_inc(newton, 1)
            dve.wait_ge(newton, n * 4 + 4)
            dve.tensor_tensor(rstd[:], inv_root[:], fix[:], ALU.mult).then_inc(rstd_ready, 1)
            dve.wait_ge(rstd_ready, n + 1)
            for s in range(SUB):
                dve.tensor_scalar(xn[:, s], x_in[:, par, s], mean_var[:, s, 0:1], rstd[:, s:s + 1],
                                  ALU.subtract, ALU.mult).then_inc(xn_ready, 1)

        @block.vector
        def _(dve):
            dve.wait_ge(mu_loaded, 16)
            dve.tensor_scalar(one_less_mu[:], mu[:], -1.0, 1.0, ALU.mult, ALU.add).then_inc(mu_ready, 1)
            token_stats(dve, 0, 0, 1)
            normalise_tokens(dve, 0, 0)
            dve.wait_ge(mu_ready, 1)
            with dve.Fori(0, B) as b:
                for c in range(NCH):
                    par = c % 2
                    n = b * NCH + c
                    dve.wait_ge(xn_t_ready, n + 1)
                    for z in range(2):
                        for cc in range(CC):
                            dve.tensor_scalar(prev_term[:, z, cc], xn_t[:, cc, 0:CH], one_less_mu[:, z, cc:cc + 1],
                                              None, ALU.mult).then_inc(prev_ready, 1)
                    for z in range(2):
                        for cc in range(CC):
                            dve.wait_ge(prev_ready, n * 4 + 2 * z + cc + 1)
                            dve.scalar_tensor_tensor(mixed[:, z, cc], xn_t[:, cc, 1:CH + 1], mu[:, z, cc:cc + 1],
                                                     prev_term[:, z, cc], ALU.mult, ALU.add).then_inc(mixed_ready, 1)
                    for j in range(2 * CC):
                        dve.wait_ge(hi_ready, n * 4 + j + 1)
                        dve.scalar_tensor_tensor(rest[:, j % 2], ps_qk[:, j % 2], SCALE if j < CC else 1.0,
                                                 parts[:, par, 0, j], ALU.mult, ALU.subtract).then_inc(rest_ready, 1)
                        dve.wait_ge(rest_ready, n * 4 + j + 1)
                        dve.tensor_copy(parts[:, par, 1, j], rest[:, j % 2]).then_inc(mid_ready, 1)
                        dve.wait_ge(mid_ready, n * 4 + j + 1)
                        dve.tensor_tensor(parts[:, par, 2, j], rest[:, j % 2], parts[:, par, 1, j],
                                          ALU.subtract).then_inc(parts_ready, 1)
                    token_stats(dve, n + 1, 1 - par, b * 2 + (c + 1) // 2 + 1)
                    dve.wait_ge(relu_ready, n + 1)
                    dve.tensor_tensor(k_act[:], relu[:], relu[:], ALU.mult).then_inc(k_act_ready, 1)
                    normalise_tokens(dve, n + 1, 1 - par)
                    dve.wait_ge(o_ready, n + 1)
                    dve.wait_ge(gate_ready, n + 1)
                    dve.wait_ge(ffn_stored[par], CREDIT * (b * 2 + c // 2 + 1))
                    dve.tensor_tensor(ffn[:, par], gate[:],
                                      ps_qk[:].rearrange("p a (s c) -> p (a s) c", c=C), ALU.mult).then_inc(gated_ready, 1)

        @block.scalar
        def _(act):
            def take_root(n):
                act.wait_ge(var_ready, n + 1)
                act.activation(root[:], var_eps[:], ACT.Sqrt).then_inc(root_ready, 1)

            take_root(0)
            act.wait_ge(setup_done, 4)
            with act.Fori(0, B) as b:
                for c in range(NCH):
                    par = c % 2
                    n = b * NCH + c
                    stores = b * 2 + c // 2
                    act.wait_ge(xt_ready, n + 1)
                    act.copy(xn_t[:, :, 0:1], zeros[:] if c == 0 else xn_t[:, :, CH:CH + 1]).then_inc(halo_ready, 1)
                    act.wait_ge(halo_ready, n + 1)
                    act.copy(xn_t[:, :, 1:CH + 1], ps_xt[:]).then_inc(xn_t_ready, 1)
                    act.wait_ge(parts_stored[par], stores * 96 + CREDIT)
                    for j in range(2 * CC):
                        act.wait_ge(qk_ready, n * 4 + j + 1)
                        act.activation(parts[:, par, 0, j], ps_qk[:, j % 2], ACT.Copy,
                                       scale=SCALE if j < CC else 1.0).then_inc(hi_ready, 1)
                    act.wait_ge(v_stored[par], stores * (SUB * 16) + CREDIT)
                    for half in range(2):
                        act.wait_ge(v_ready, n * 2 + half + 1)
                        act.copy(v_pad[:, par, 2 * half:2 * half + 2, :, 0:HD],
                                 ps_v[:, 2 * half:2 * half + 2].rearrange("p s (h d) -> p s h d", d=HD)).then_inc(v_pad_ready, 1)
                    act.wait_ge(r_ready, n + 1)
                    act.activation(gate[:], ps_r[:], ACT.Sigmoid).then_inc(gate_ready, 1)
                    act.wait_ge(kt_ready, n + 1)
                    act.activation(relu[:], ps_xt[:], ACT.Relu).then_inc(relu_ready, 1)
                    take_root(n + 1)

        @block.tensor
        def _(pe):
            pe.wait_ge(consts_ready, 2)
            pe.wait_ge(weights_loaded, 16 * 5)
            with pe.Fori(0, B) as b:
                for c in range(NCH):
                    n = b * NCH + c
                    pe.wait_ge(xn_ready, n * SUB + SUB)
                    for cc in range(CC):
                        for s in range(SUB):
                            last = pe.transpose(ps_xt[:, cc, s * P:(s + 1) * P], xn[:, s, cc * P:(cc + 1) * P], ident[:])
                    last.then_inc(xt_ready, 1)
                    pe.wait_ge(xn_t_ready, n + 1)
                    for j in range(2 * CC):
                        if j >= 2:
                            pe.wait_ge(rest_ready, n * 4 + j - 1)
                        elif c > 0:
                            pe.wait_ge(gated_ready, n)
                        for cc in range(CC):
                            last = pe.matmul(ps_qk[:, j % 2], w_in_sb[:, cc, j * P:(j + 1) * P],
                                             xn_t[:, cc, 1:CH + 1], start=(cc == 0), stop=(cc == CC - 1))
                        last.then_inc(qk_ready, 1)
                    for s in range(SUB):
                        for cc in range(CC):
                            last = pe.matmul(ps_v[:, s], xn_t[:, cc, 1 + s * P:1 + (s + 1) * P],
                                             w_in_sb[:, cc, 2 * C:3 * C], start=(cc == 0), stop=(cc == CC - 1))
                        if s % 2:
                            last.then_inc(v_ready, 1)
                    pe.wait_ge(mixed_ready, n * 4 + 2)
                    for s in range(SUB):
                        for cc in range(CC):
                            last = pe.matmul(ps_r[:, s], mixed[:, 0, cc, s * P:(s + 1) * P], w_r_sb[:, cc],
                                             start=(cc == 0), stop=(cc == CC - 1))
                    last.then_inc(r_ready, 1)
                    pe.wait_ge(mixed_ready, n * 4 + 4)
                    for m in range(CC):
                        for cc in range(CC):
                            last = pe.matmul(ps_xt[:, m], w_k_sb[:, cc, m * P:(m + 1) * P], mixed[:, 1, cc],
                                             start=(cc == 0), stop=(cc == CC - 1))
                    last.then_inc(kt_ready, 1)
                    pe.wait_ge(v_pad_ready, n * 2 + 2)
                    pe.wait_ge(gate_ready, n + 1)
                    pe.wait_ge(parts_ready, n * 4 + 4)
                    pe.wait_ge(k_act_ready, n + 1)
                    for s in range(SUB):
                        for m in range(CC):
                            last = pe.matmul(ps_qk[:, s // 2, (s % 2) * C:(s % 2 + 1) * C],
                                             k_act[:, m, s * P:(s + 1) * P], w_v_sb[:, m],
                                             start=(m == 0), stop=(m == CC - 1))
                    last.then_inc(o_ready, 1)
                pe.wait_ge(gated_ready, b * NCH + NCH)


def stage_attention(nc, parts_d, vpad_d, ident, ident16, attn_t):
    with ExitStack() as ctx:
        def sb(name, shape, dt=F32):
            return ctx.enter_context(nc.sbuf_tensor(name, shape, dt))

        def ps(name, shape):
            return ctx.enter_context(nc.psum_tensor(name, shape, F32))

        def sem(name):
            return ctx.enter_context(nc.semaphore(name))

        q_op = sb("q_op", [P, 2, GH, T], BF16)
        k_op = sb("k_op", [P, 2, GH, T], BF16)
        v_sb = sb("v_sb", [P, 2, NT, GH * HW])
        after = sb("after", [P, NT, GH, HD])
        v_after = sb("v_after", [P, 2, NT, GH * HW])
        keys_after = sb("keys_after", [P, P])
        ones = sb("ones", [P, P])
        mask16 = sb("mask16", [P, P], BF16)
        floor = sb("floor", [P, GH, NT])
        probs = sb("probs", [P, PRING, CH])
        part_max = sb("part_max", [P, 2, GH * SUB, NCH])
        raw_max = sb("raw_max", [P, GH, SUB])
        row_max = sb("row_max", [P, NCH, GH, SUB])
        shift_rest = sb("shift_rest", [P, GH, SUB])
        shift = sb("shift", [P, NCH, SUB, 3, GH], BF16)
        shift_t = sb("shift_t", [3 * GH, 2, CH], BF16)
        masked_weight = sb("masked_weight", [P, NCH, GH * SUB])
        diag_weight = sb("diag_weight", [P, 2, GH * SUB, P])
        sums = sb("sums", [P, 2, CH])
        turned = sb("turned", [P, CH])
        inv_denom = sb("inv_denom", [P, CH // HW])
        normed = sb("normed", [P, 2, CH])

        ps_s = ps("ps_s", [P, SRING, CH])
        ps_m = ps("ps_m", [P, MRING, CH])
        ps_o = ps("ps_o", [P, CH])
        ps_x = ps("ps_x", [P, CH])
        ps_shift = ps_x[:].bitcast(BF16)

        consts_set, consts_made = sem("consts_set"), sem("consts_made")
        q_loaded = [sem("q_loaded0"), sem("q_loaded1")]
        k_loaded = [sem("k_loaded0"), sem("k_loaded1")]
        v_loaded = [sem("v_loaded0"), sem("v_loaded1")]
        piece_ready, piece_reduced = sem("piece_ready"), sem("piece_reduced")
        raw_ready, max_ready, hi_ready, rest_ready, mid_ready, shift_ready = (
            sem("raw_ready"), sem("max_ready"), sem("shift_hi_ready"), sem("shift_rest_ready"),
            sem("shift_mid_ready"), sem("shift_ready"))
        shift_turned, shift_t_ready = sem("shift_turned"), sem("shift_t_ready")
        shift_loaded = [sem("shift_loaded0"), sem("shift_loaded1")]
        weight_ready, diag_ready = sem("weight_ready"), sem("diag_ready")
        after_ready, suffix_ready, v_after_ready = sem("after_ready"), sem("suffix_ready"), sem("v_after_ready")
        scores_ready, probs_ready, probs_masked, probs_used = (
            sem("scores_ready"), sem("probs_ready"), sem("probs_masked"), sem("probs_used"))
        out_ready, sums_ready, turned_ready, denom_ready, divided, normed_ready = (
            sem("out_ready"), sem("sums_ready"), sem("turned_ready"), sem("denom_ready"),
            sem("divided"), sem("normed_ready"))
        normed_stored = [sem("normed_stored0"), sem("normed_stored1")]
        passed = sem("passed_mask")
        LOADS = len(Q_PARTS) * 16
        SHIFTS = 3 * 16
        STORES = GH * 16
        USED = PRING // GH
        block = ctx.enter_context(nc.Block())

        parts_in = parts_d.rearrange("r (z b) (cc g h d) t -> r z (b cc) g d h t", b=B, cc=CC, g=2, h=GH)
        v_in = vpad_d.rearrange("(i g) p t f -> i g p t f", g=2)

        def unit_of(i, p, u):
            return (i * 2 + p) * NCH + u

        @block.sync
        def _(sp):
            def load_group(i, p):
                for r in range(len(Q_PARTS)):
                    rows = slice(r * HD, (r + 1) * HD)
                    sp.dma_start(q_op[rows, p], parts_in[Q_PARTS[r], 0, i, p]).then_inc(q_loaded[p], 16)
                    sp.dma_start(k_op[rows, p], parts_in[K_PARTS[r], 1, i, p]).then_inc(k_loaded[p], 16)
                sp.dma_start(v_sb[:, p], v_in[i, p]).then_inc(v_loaded[p], 16)

            def place_shift(p, u, n):
                sp.wait_ge(shift_t_ready, n + 1)
                for part in range(3):
                    sp.dma_start(q_op[ROWS + part:ROWS + part + 1, p, :, u * CH:(u + 1) * CH],
                                 shift_t[part * GH:(part + 1) * GH, u % 2]).then_inc(shift_loaded[u % 2], 16)

            def keep_normed(i, p, u):
                sp.wait_ge(normed_ready, unit_of(i, p, u) + 3)
                for h in range(GH):
                    row = (p * GH + h) * HD
                    sp.dma_start(attn_t[row:row + HD, i, u * CH:(u + 1) * CH],
                                 normed[h * HW:h * HW + HD, u % 2]).then_inc(normed_stored[u % 2], 16)

            def group(i, p, last):
                if p == 1:
                    keep_normed(i, 0, NCH - 1)
                if not last:
                    sp.wait_ge(out_ready, unit_of(i, p, 0) + 1)
                    load_group(i + p, 1 - p)
                place_shift(p, 2, unit_of(i, p, 2))
                keep_normed(i, p, 0)
                keep_normed(i, p, 1)
                place_shift(p, 3, unit_of(i, p, 3))
                keep_normed(i, p, 2)
                if not last:
                    place_shift(1 - p, 0, unit_of(i, p, NCH))
                    place_shift(1 - p, 1, unit_of(i, p, NCH + 1))
                if p == 1:
                    keep_normed(i, 1, NCH - 1)

            load_group(0, 0)
            sp.sem_inc(piece_reduced, MRING)
            sp.sem_inc(probs_ready, SRING)
            sp.sem_inc(probs_used, USED)
            sp.sem_inc(out_ready, 1)
            sp.sem_inc(sums_ready, 1)
            sp.sem_inc(normed_ready, 2)
            for half in range(2):
                sp.sem_inc(normed_stored[half], STORES)
                sp.sem_inc(shift_loaded[half], SHIFTS)
            place_shift(0, 0, 0)
            place_shift(0, 1, 1)
            with sp.Fori(0, B * CC - 1) as i:
                group(i, 0, False)
                group(i, 1, False)
            group(B * CC - 1, 0, False)
            group(B * CC - 1, 1, True)
            for s in normed_stored:
                sp.wait_ge(s, STORES * (1 + B * NG * NCH // 2))

        @block.gpsimd
        def _(pool):
            pool.memset(ones[:], 1.0).then_inc(consts_set, 1)
            pool.memset(mask16[:], 0.0).then_inc(consts_set, 1)
            pool.memset(floor[:], 0.0).then_inc(consts_set, 1)
            pool.memset(after[:, NT - 1], 0.0).then_inc(consts_set, 1)
            pool.wait_ge(consts_set, 4)
            pool.memset(k_op[ROWS:KROWS], 1.0).then_inc(consts_set, 1)
            pool.wait_ge(consts_set, 5)
            pool.affine_select(out=keys_after[:], in_=ones[:], compare_op=ALU.is_gt, fill=0.0, base=0,
                               pattern=[[-1, P]], channel_multiplier=1).then_inc(consts_made, 1)
            pool.affine_select(out=mask16[:], in_=mask16[:], compare_op=ALU.is_ge, fill=NEG, base=0,
                               pattern=[[-1, P]], channel_multiplier=1).then_inc(consts_made, 1)
            pool.affine_select(out=floor[:, :, NT - 1], in_=floor[:, :, NT - 1], compare_op=ALU.not_equal, fill=LOWEST,
                               base=-(P - 1), pattern=[[0, GH]], channel_multiplier=1).then_inc(consts_made, 1)
            for half in range(2):
                counts = v_after[:, half].rearrange("p t (h w) -> p t h w", w=HW)[:, :, :, HD:HW]
                pool.iota(counts, pattern=[[-P, NT], [0, GH], [0, HW - HD]], base=T - 1, channel_multiplier=-1,
                          allow_small_or_imprecise_dtypes=True).then_inc(consts_made, 1)

            def add_up_after(p, n, loads):
                pool.wait_ge(v_loaded[p], 16 * loads)
                values = v_sb[:, p].rearrange("p t (h w) -> p t h w", w=HW)
                for j in range(NT - 2, -1, -1):
                    if j < NT - 2:
                        pool.wait_ge(after_ready, n * (NT - 1) + NT - 2 - j)
                    pool.tensor_tensor(after[:, j], after[:, j + 1], values[:, j + 1, :, 0:HD], ALU.add).then_inc(after_ready, 1)

            def spread_weight(u, n):
                pool.wait_ge(weight_ready, n + 1)
                if not isinstance(n, int):
                    pool.wait_ge(out_ready, n)
                pool.tensor_tensor(diag_weight[:, u % 2], ident[:].unsqueeze(1).broadcast_to([P, GH * SUB, P]),
                                   masked_weight[:, u].unsqueeze(2).broadcast_to([P, GH * SUB, P]),
                                   ALU.mult).then_inc(diag_ready, 1)

            def group(i, p, last):
                G = i * 2 + p
                for u in range(NCH):
                    if u == 2 and not last:
                        pool.wait_ge(v_after_ready, G * 4 + 4)
                        add_up_after(1 - p, G + 1, i + 1 + p)
                    for kt in range(SUB * u, SUB * u + SUB):
                        for h in range(GH):
                            slot = (KT0[u] + kt) * GH + h
                            pool.wait_ge(probs_ready, G * SLOTS + slot + 1 + SRING)
                            pool.sem_inc(passed, 1)
                            blk = probs[:, slot % PRING, 0:P]
                            pool.affine_select(out=blk, in_=blk, compare_op=ALU.is_ge, fill=0.0, base=0,
                                               pattern=[[1, P]], channel_multiplier=-1).then_inc(probs_masked, 1)
                    if not (u == NCH - 1 and last):
                        spread_weight((u + 1) % NCH, unit_of(i, p, u + 1))

            add_up_after(0, 0, 1)
            spread_weight(0, 0)
            with pool.Fori(0, B * CC - 1) as i:
                group(i, 0, False)
                group(i, 1, False)
            group(B * CC - 1, 0, False)
            group(B * CC - 1, 1, True)

        @block.scalar
        def _(act):
            def weight(n, u):
                act.wait_ge(max_ready, n + 1)
                act.activation(masked_weight[:, u], row_max[:, u].rearrange("p h s -> p (h s)"), ACT.Exp,
                               scale=-1.0).then_inc(weight_ready, 1)

            def keep_suffix(p, quad, n):
                act.wait_ge(suffix_ready, n + 1)
                act.copy(v_after[:, p, quad * SUB:(quad + 1) * SUB].rearrange("p s (h w) -> p (s h) w", w=HW)[:, :, 0:HD],
                         ps_x[:, 0:SUB * GH * HD].rearrange("p (f d) -> p f d", d=HD)).then_inc(v_after_ready, 1)

            def keep_shift(u, n, earlier):
                act.wait_ge(shift_turned, n + 1)
                act.wait_ge(shift_loaded[u % 2], (earlier + 1) * SHIFTS)
                act.copy(shift_t[:, u % 2], ps_shift[0:3 * GH, 0:CH]).then_inc(shift_t_ready, 1)

            def keep_sums(n, par):
                act.wait_ge(out_ready, n + 2)
                act.wait_ge(normed_ready, n + 1)
                act.copy(sums[:, par], ps_o[:]).then_inc(sums_ready, 1)

            def group(i, p, last):
                G = i * 2 + p
                for u in range(NCH):
                    nxt = NCH if u == NCH - 1 else 0
                    for kt in range(key_tiles(u)):
                        width = CH - first_query(u, kt)
                        act.wait_ge(probs_used, G * KTILES + KT0[u] + kt + 1)
                        for h in range(GH):
                            slot = (KT0[u] + kt) * GH + h
                            act.wait_ge(scores_ready, G * SLOTS + slot + 1)
                            act.activation(probs[:, slot % PRING, 0:width], ps_s[:, slot % SRING, 0:width],
                                           ACT.Exp).then_inc(probs_ready, 1)
                        if kt == 0 and (u > 0 or p == 1):
                            keep_sums(unit_of(i, p, u - 1), (u - 1) % 2)
                        if (u, kt) in SV_AT and not last:
                            keep_suffix(1 - p, SV_AT[u, kt], (G + 1) * 4 + SV_AT[u, kt])
                        if (u, kt) in SHIFT_AT and not (nxt and last):
                            v = SHIFT_AT[u, kt]
                            weight(unit_of(i, p, v + nxt), v)
                            keep_shift(v, unit_of(i, p, v + nxt), (G + (nxt > 0)) * (NCH // 2) + v // 2)
                if p == 1:
                    keep_sums(unit_of(i, 1, NCH - 1), 1)

            act.wait_ge(consts_made, 5)
            for quad in range(4):
                keep_suffix(0, quad, quad)
            for u in range(2):
                weight(u, u)
                keep_shift(u, u, 0)
            with act.Fori(0, B * CC - 1) as i:
                group(i, 0, False)
                group(i, 1, False)
            group(B * CC - 1, 0, False)
            group(B * CC - 1, 1, True)

        @block.vector
        def _(dve):
            dve.wait_ge(consts_made, 3)

            def reduce_piece(f, base):
                u, h, s, pc, width = piece(f)
                dve.wait_ge(piece_ready, base + f + 1)
                dve.tensor_reduce(part_max[:, u % 2, h * SUB + s, pc:pc + 1], ps_m[:, f % MRING, 0:width], AX_X,
                                  ALU.max).then_inc(piece_reduced, 1)

            def max_step(k, u, n, reduced):
                by_head = [shift[:, u, :, part].rearrange("p s h -> p h s") for part in range(3)]
                if k == 0:
                    dve.wait_ge(piece_reduced, reduced + MRING)
                    dve.tensor_reduce(raw_max[:].rearrange("p h s -> p (h s)"), part_max[:, u % 2, :, 0:u + 1], AX_X,
                                      ALU.max).then_inc(raw_ready, 1)
                if k == 1:
                    dve.wait_ge(raw_ready, n + 1)
                    dve.tensor_tensor(row_max[:, u], raw_max[:], floor[:, :, u * SUB:(u + 1) * SUB],
                                      ALU.max).then_inc(max_ready, 1)
                if k == 2:
                    dve.wait_ge(max_ready, n + 1)
                    dve.tensor_scalar(by_head[0], row_max[:, u], -1.0, None, ALU.mult).then_inc(hi_ready, 1)
                if k == 3:
                    dve.wait_ge(hi_ready, n + 1)
                    dve.scalar_tensor_tensor(shift_rest[:], row_max[:, u], -1.0, by_head[0], ALU.mult,
                                             ALU.subtract).then_inc(rest_ready, 1)
                if k == 4:
                    dve.wait_ge(rest_ready, n + 1)
                    dve.tensor_copy(by_head[1], shift_rest[:]).then_inc(mid_ready, 1)
                if k == 5:
                    dve.wait_ge(mid_ready, n + 1)
                    dve.tensor_tensor(by_head[2], shift_rest[:], by_head[1], ALU.subtract).then_inc(shift_ready, 1)

            def norm_step(k, n, par, stored):
                blocks = turned[:].rearrange("p (b w) -> p b w", w=HW)
                if k == 0:
                    dve.wait_ge(normed_ready, n + 2)
                    dve.wait_ge(sums_ready, n + 2)
                    dve.transpose(turned[:], sums[:, par]).then_inc(turned_ready, 1)
                if k == 1:
                    dve.wait_ge(turned_ready, n + 1)
                    dve.reciprocal(inv_denom[:], blocks[:, :, HD]).then_inc(denom_ready, 1)
                if k == 2:
                    dve.wait_ge(denom_ready, n + 1)
                    dve.tensor_tensor(blocks[:, :, 0:HD], blocks[:, :, 0:HD],
                                      inv_denom[:].unsqueeze(2).broadcast_to([P, CH // HW, HD]), ALU.mult).then_inc(divided, 1)
                if k == 3:
                    dve.wait_ge(divided, n + 1)
                    dve.wait_ge(normed_stored[par], (stored + 1) * STORES)
                    dve.transpose(normed[:, par], turned[:]).then_inc(normed_ready, 1)

            def after_piece(f, n0, base, close):
                for u in range(NCH):
                    k = f + 1 - PIECE0[u + 1]
                    if k == 0 and close:
                        for step in range(MAX_STEPS):
                            max_step(step, u, n0 + u, base + PIECE0[u + 1])
                    elif 0 <= k < MAX_STEPS and not (u == NCH - 1 or close):
                        max_step(k, u, n0 + u, base + PIECE0[u + 1])

            def group(i, p, last):
                G = i * 2 + p
                for u in range(NCH):
                    nxt = NCH if u == NCH - 1 else 0
                    base = (G + (nxt > 0)) * PIECES
                    for hs in range(key_tiles(u) * GH):
                        if not (nxt and last):
                            for f in pieces_of(u, hs):
                                reduce_piece(f, base)
                                after_piece(f, unit_of(i, p, nxt), base, f + 1 == PIECES)
                        if NORM_AT <= hs < NORM_AT + NORM_STEPS and (u > 0 or p == 1):
                            norm_step(hs - NORM_AT, unit_of(i, p, u - 1), (u - 1) % 2,
                                      G * (NCH // 2) + (u - 1) // 2)
                if p == 1:
                    for k in range(NORM_STEPS):
                        norm_step(k, unit_of(i, 1, NCH - 1), 1, G * (NCH // 2) + (NCH - 1) // 2)

            for f in range(HEAD_START):
                reduce_piece(f, 0)
                after_piece(f, 0, 0, False)
            with dve.Fori(0, B * CC - 1) as i:
                group(i, 0, False)
                group(i, 1, False)
            group(B * CC - 1, 0, False)
            group(B * CC - 1, 1, True)

        @block.tensor
        def _(pe):
            pe.wait_ge(consts_made, 5)

            def score_piece(f, p, base):
                u, h, s, pc, width = piece(f)
                pe.wait_ge(piece_reduced, base + f + 1)
                q0 = u * CH + s * P
                last = pe.matmul(ps_m[:, f % MRING, 0:width], q_op[0:ROWS, p, h, q0:q0 + P],
                                 k_op[0:ROWS, p, h, pc * CH:pc * CH + width], start=True, stop=(pc < u))
                if pc == u:
                    last = pe.matmul(ps_m[:, f % MRING, s * P:width], ident16[:], mask16[:], start=False, stop=True)
                last.then_inc(piece_ready, 1)

            def turn_shift(u, n, quads):
                pe.wait_ge(shift_ready, n + 1)
                if not isinstance(n, int) or n > 0:
                    pe.wait_ge(shift_t_ready, n)
                pe.wait_ge(v_after_ready, quads)
                for s in range(SUB):
                    last = pe.transpose(ps_shift[0:3 * GH, s * P:(s + 1) * P],
                                        shift[:, u, s].rearrange("p r h -> p (r h)"), ident16[:])
                last.then_inc(shift_turned, 1)

            def sum_suffix(p, quad, n, turned_before):
                pe.wait_ge(after_ready, (n + 1) * (NT - 1))
                if not isinstance(n, int) or quad > 0:
                    pe.wait_ge(v_after_ready, n * 4 + quad)
                if not isinstance(turned_before, int):
                    pe.wait_ge(shift_t_ready, turned_before)
                tiles = slice(quad * SUB, (quad + 1) * SUB)
                values = v_sb[:, p, tiles].rearrange("p s (h w) -> p (s h) w", w=HW)[:, :, 0:HD]
                width = SUB * GH * HD
                pe.matmul(ps_x[:, 0:width], keys_after[:], values, start=True, stop=False)
                pe.matmul(ps_x[:, 0:width], ones[:], after[:, tiles].rearrange("p s h d -> p (s h d)"),
                          start=False, stop=True).then_inc(suffix_ready, 1)

            def score_tile(p, u, kt, h, G):
                slot = (KT0[u] + kt) * GH + h
                q0 = first_query(u, kt)
                pe.wait_ge(probs_ready, G * SLOTS + slot + 1)
                pe.matmul(ps_s[:, slot % SRING, 0:CH - q0], k_op[0:KROWS, p, h, kt * P:(kt + 1) * P],
                          q_op[0:KROWS, p, h, u * CH + q0:(u + 1) * CH], start=True, stop=True).then_inc(scores_ready, 1)

            def weigh_values(p, u, kt, G):
                n = G * NCH + u
                if kt == 0:
                    pe.wait_ge(sums_ready, n + 1)
                if kt < SUB * u:
                    pe.wait_ge(probs_ready, G * SLOTS + (KT0[u] + kt + 1) * GH + SRING)
                else:
                    pe.wait_ge(probs_masked, n * (SUB * GH) + (kt - SUB * u + 1) * GH)
                q0 = first_query(u, kt)
                for h in range(GH):
                    last = pe.matmul(ps_o[h * HW:(h + 1) * HW, q0:CH], v_sb[:, p, kt, h * HW:(h + 1) * HW],
                                     probs[:, ((KT0[u] + kt) * GH + h) % PRING, 0:CH - q0], start=(kt == 0), stop=False)
                last.then_inc(probs_used, 1)

            def masked_keys(p, u, G):
                pe.wait_ge(diag_ready, G * NCH + u + 1)
                pe.wait_ge(v_after_ready, G * 4 + 4)
                for s in range(SUB):
                    for h in range(GH):
                        last = pe.matmul(ps_o[h * HW:(h + 1) * HW, s * P:(s + 1) * P],
                                         v_after[:, p, u * SUB + s, h * HW:(h + 1) * HW],
                                         diag_weight[:, u % 2, h * SUB + s], start=False, stop=(s == SUB - 1))
                last.then_inc(out_ready, 1)

            def finish_unit(p, u, G):
                weigh_values(p, u, key_tiles(u) - 1, G)
                masked_keys(p, u, G)

            def group(i, p, last):
                G = i * 2 + p
                pe.wait_ge(q_loaded[p], (i + 1) * LOADS)
                pe.wait_ge(k_loaded[p], (i + 1) * LOADS)
                for u in range(NCH):
                    nxt = NCH if u == NCH - 1 else 0
                    pe.wait_ge(shift_loaded[u % 2], (G * (NCH // 2) + u // 2 + 2) * SHIFTS)
                    if nxt and not last:
                        pe.wait_ge(q_loaded[1 - p], (i + 1 + p) * LOADS)
                        pe.wait_ge(k_loaded[1 - p], (i + 1 + p) * LOADS)
                    for kt in range(key_tiles(u)):
                        for h in range(GH):
                            score_tile(p, u, kt, h, G)
                            if not (nxt and last):
                                for f in pieces_of(u, kt * GH + h):
                                    score_piece(f, 1 - p if nxt else p, (G + (nxt > 0)) * PIECES)
                            if h == 1:
                                if kt > 0:
                                    weigh_values(p, u, kt - 1, G)
                                elif u > 0:
                                    finish_unit(p, u - 1, G)
                                elif p == 1:
                                    finish_unit(0, NCH - 1, i * 2)
                        if (u, kt) in SV_AT and not last:
                            sum_suffix(1 - p, SV_AT[u, kt], G + 1,
                                       unit_of(i, p, NCH + sum(a == u and b < kt for a, b in SHIFT_AT)))
                        if (u, kt) in SHIFT_AT and not (nxt and last):
                            v = SHIFT_AT[u, kt]
                            quads = (G + 1) * 4 + (sum(b < kt for _, b in SV_AT) if nxt else 0)
                            turn_shift(v, unit_of(i, p, v + nxt), quads)
                if p == 1:
                    finish_unit(1, NCH - 1, G)

            pe.wait_ge(q_loaded[0], LOADS)
            pe.wait_ge(k_loaded[0], LOADS)
            pe.wait_ge(v_loaded[0], 16)
            for quad in range(4):
                sum_suffix(0, quad, 0, 0)
            for f in range(HEAD_START):
                score_piece(f, 0, 0)
                for u in range(2):
                    if f == PIECE0[u + 1] + MAX_STEPS + 2:
                        turn_shift(u, u, 4)
            with pe.Fori(0, B * CC - 1) as i:
                group(i, 0, False)
                group(i, 1, False)
            group(B * CC - 1, 0, False)
            group(B * CC - 1, 1, True)


def stage_output(nc, ffn_d, ident, w_out_sb, attn_t, out):
    with ExitStack() as ctx:
        def sb(name, shape, dt=F32):
            return ctx.enter_context(nc.sbuf_tensor(name, shape, dt))

        def sem(name):
            return ctx.enter_context(nc.semaphore(name))

        ffn = sb("ffn_in", [P, 2, SUB, C])
        attn = sb("attn_chunk", [P, 2, CC, CH])
        total = sb("total", [P, 2, SUB, C])
        ps_y = ctx.enter_context(nc.psum_tensor("ps_y", [P, 2, SUB, C], F32))
        ffn_loaded = [sem("ffn_loaded0"), sem("ffn_loaded1")]
        out_stored = [sem("out_stored0"), sem("out_stored1")]
        attn_ready, y_ready, total_ready = sem("attn_ready"), sem("y_ready"), sem("total_ready")
        ffn_tiles = ffn_d.rearrange("(n s p) c -> n p s c", s=SUB, p=P)
        out_tiles = out.rearrange("(n s p) c -> n p s c", s=SUB, p=P)
        block = ctx.enter_context(nc.Block())

        @block.sync
        def _(sp):
            sp.sem_inc(y_ready, 2)
            sp.sem_inc(total_ready, 2)
            sp.sem_inc(out_stored[0], 16)
            sp.sem_inc(out_stored[1], 16)
            with sp.Fori(0, B) as b:
                for c in range(NCH):
                    sp.wait_ge(total_ready, b * NCH + c + 3)
                    sp.dma_start(out_tiles[b * NCH + c], total[:, c % 2]).then_inc(out_stored[c % 2], 16)
            for s in out_stored:
                sp.wait_ge(s, 16 + B * 2 * 16)

        @block.scalar
        def _(act):
            with act.Fori(0, B) as b:
                for c in range(NCH):
                    act.wait_ge(y_ready, b * NCH + c + 1)
                    act.copy(attn[:, c % 2], attn_t[:, bass.ds(b * CC, CC), c * CH:(c + 1) * CH]).then_inc(attn_ready, 1)

        @block.tensor
        def _(pe):
            with pe.Fori(0, B) as b:
                for c in range(NCH):
                    pe.wait_ge(attn_ready, b * NCH + c + 1)
                    pe.wait_ge(total_ready, b * NCH + c + 1)
                    for s in range(SUB):
                        for cc in range(CC):
                            last = pe.matmul(ps_y[:, c % 2, s], attn[:, c % 2, cc, s * P:(s + 1) * P],
                                             w_out_sb[:, cc], start=(cc == 0), stop=(cc == CC - 1))
                    last.then_inc(y_ready, 1)

        @block.vector
        def _(dve):
            with dve.Fori(0, B) as b:
                for c in range(NCH):
                    dve.wait_ge(ffn_loaded[c % 2], (b * 2 + c // 2 + 1) * 16)
                    dve.wait_ge(y_ready, b * NCH + c + 3)
                    dve.wait_ge(out_stored[c % 2], (b * 2 + c // 2) * 16 + 16)
                    dve.tensor_tensor(total[:, c % 2], ffn[:, c % 2], ps_y[:, c % 2], ALU.add).then_inc(total_ready, 1)

        @block.gpsimd
        def _(pool):
            with pool.Fori(0, B) as b:
                for c in range(NCH):
                    pool.wait_ge(total_ready, b * NCH + c + 1)
                    pool.dma_start(ffn[:, c % 2], ffn_tiles[b * NCH + c]).then_inc(ffn_loaded[c % 2], 16)


def kernel(L0_attn_x, L0_attn_w_in, L0_attn_w_out, L0_ffn_W_r, L0_ffn_W_k, L0_ffn_W_v, L0_ffn_mu_r, L0_ffn_mu_k):
    import numpy as np
    import concourse.bacc as bacc
    from concourse.bass_utils import run_bass_kernel_spmd

    def laid(a, turn=False):
        a = np.asarray(a)
        return np.ascontiguousarray(a.T if turn else a)

    inputs = {
        "x": laid(L0_attn_x).reshape(B * T, C),
        "w_in_t": laid(L0_attn_w_in, True),
        "w_r_t": laid(L0_ffn_W_r, True),
        "w_k_t": laid(L0_ffn_W_k, True),
        "w_v_t": laid(L0_ffn_W_v, True),
        "w_out_t": laid(L0_attn_w_out, True),
        "mu_rk": laid(np.stack([np.asarray(L0_ffn_mu_r), np.asarray(L0_ffn_mu_k)]).reshape(2, CC, P).transpose(2, 0, 1)),
    }
    nc = bacc.Bacc("TRN2", target_bir_lowering=False, num_devices=1)
    nc.disable_value_cache = True
    args = [nc.dram_tensor(name, a.shape, F32, kind="ExternalInput").ap() for name, a in inputs.items()]
    y = nc.dram_tensor("y", (B * T, C), F32, kind="ExternalOutput").ap()
    build(nc, *args, y)
    r = run_bass_kernel_spmd(nc, [inputs], core_ids=[0])
    return r.results[0]["y"].reshape(B, T, C)
```

```python
from contextlib import ExitStack

import concourse.bass as bass
from concourse import mybir

F32 = mybir.dt.float32
BF16 = mybir.dt.bfloat16
ALU = mybir.AluOpType
ACT = mybir.ActivationFunctionType
AX_X = mybir.AxisListType.X

P = 128
B, T, C = 2, 2048, 256
H, HD = 16, 16
SCALE = 0.25
EPS = 1e-5
CC = C // P
CH = 512
NCH = T // CH
SUB = CH // P
NT = T // P
GH = 4
NG = H // GH
HW = 32
NEG = -1e30
LOWEST = -3e38

Q_PARTS = (0, 1, 2, 0, 1, 0)
K_PARTS = (0, 0, 0, 1, 1, 2)
ROWS = HD * len(Q_PARTS)
KROWS = ROWS + 3

PIECE0 = [SUB * GH * u * (u + 1) // 2 for u in range(NCH + 1)]
PIECES = PIECE0[NCH]
HEAD_START = PIECE0[2] + 32
SLOT_PIECES = {0: (HEAD_START, PIECE0[3]), 1: (PIECE0[3], PIECE0[3] + 32),
               2: (PIECE0[3] + 32, PIECES), 3: (0, HEAD_START)}
SLOT_SPREAD = {0: 16, 1: 32, 2: 30, 3: 64}
TOKEN_STEPS = 12
PIECES_FROM = 8
PIECES_BEHIND = 10
SHIFT_AT = {(3, 5): 0, (3, 11): 1, (1, 2): 2, (2, 8): 3}
SV_AT = {(3, 2): 0, (3, 4): 1, (3, 7): 2, (3, 9): 3}
FIRST_SV_AT = {(0, 0): 0, (0, 1): 1, (0, 2): 2, (0, 3): 3}
MAX_STEPS = 6
NORM_STEPS = 4
LAG = 2
NORM_AT = GH * LAG + 1
KT0 = [SUB * u * (u + 1) // 2 for u in range(NCH + 1)]
KTILES = KT0[NCH]
SLOTS = KTILES * GH
OUT_AT = {**{(2, 8 + k): k for k in range(4)}, **{(3, k): 4 + k for k in range(16)}}
OUTS = B * NT
OUT_CHUNKS = len(OUT_AT) // SUB
ORING = 4
PRING = 16
SRING = 3
MRING = 3


def piece(f):
    u = max(v for v in range(NCH) if PIECE0[v] <= f)
    hs, pc = divmod(f - PIECE0[u], u + 1)
    h, s = divmod(hs, SUB)
    return u, h, s, pc, (CH if pc < u else P * (s + 1))


def pieces_of(slot, head_step):
    lo, hi = SLOT_PIECES[slot]
    n, spread = hi - lo, SLOT_SPREAD[slot]
    at = min(head_step, spread)
    return range(lo + n * at // spread, lo + n * min(at + 1, spread) // spread)


def pieces_beside_tokens(c, step):
    done = c * TOKEN_STEPS + step - PIECES_FROM
    steps = NCH * TOKEN_STEPS - PIECES_FROM
    beside = HEAD_START - PIECES_BEHIND
    return range(beside * max(0, done) // steps, beside * max(0, done + 1) // steps)


def key_tiles(u):
    return SUB * (u + 1)


def first_query(u, kt):
    return P * max(0, kt - SUB * u)


def build(nc, x, w_in_t, w_r_t, w_k_t, w_v_t, w_out_t, mu_rk, out):
    parts_d = nc.dram_tensor("parts_d", [3, 2 * B, C, T], BF16, kind="Internal").ap()
    vpad_d = nc.dram_tensor("vpad_d", [B * NG, P, NT, GH * HW], F32, kind="Internal").ap()
    ffn_d = nc.dram_tensor("ffn_d", [B * T, C], F32, kind="Internal").ap()

    with ExitStack() as whole:
        ident = whole.enter_context(nc.sbuf_tensor("ident", [P, P], F32))
        ident16 = whole.enter_context(nc.sbuf_tensor("ident16", [P, P], BF16))
        w_out_sb = whole.enter_context(nc.sbuf_tensor("w_out_sb", [P, CC, C], F32))
        consts_ready = whole.enter_context(nc.semaphore("consts_ready"))
        ops = Operands(nc, whole, parts_d, vpad_d, ident16)
        stage_tokens(nc, x, w_in_t, w_r_t, w_k_t, w_v_t, w_out_t, mu_rk,
                     parts_d, vpad_d, ffn_d, ident, ident16, w_out_sb, consts_ready, ops)
        attn_t = whole.enter_context(nc.sbuf_tensor("attn_t", [P, B * CC, T], F32))
        stage_attention(nc, ops, ident, ident16, attn_t, ffn_d, w_out_sb, out)


class Operands:

    def __init__(self, nc, ctx, parts_d, vpad_d, ident16):
        def sb(name, shape, dt=F32):
            return ctx.enter_context(nc.sbuf_tensor(name, shape, dt))

        def sem(name):
            return ctx.enter_context(nc.semaphore(name))

        self.LOADS = len(Q_PARTS) * 16
        self.ident16 = ident16
        self.q_op = sb("q_op", [P, 2, GH, T], BF16)
        self.k_op = sb("k_op", [P, 2, GH, T], BF16)
        self.v_sb = sb("v_sb", [P, 2, NT, GH * HW])
        self.after = sb("after", [P, NT, GH, HD])
        self.v_after = sb("v_after", [P, 2, NT, GH * HW])
        self.keys_after = sb("keys_after", [P, P])
        self.ones = sb("ones", [P, P])
        self.mask16 = sb("mask16", [P, P], BF16)
        self.floor = sb("floor", [P, GH, NT])
        self.part_max = sb("part_max", [P, 2, GH * SUB, NCH])
        self.raw_max = sb("raw_max", [P, GH, SUB])
        self.row_max = sb("row_max", [P, NCH, GH, SUB])
        self.shift_rest = sb("shift_rest", [P, GH, SUB])
        self.shift = sb("shift", [P, NCH, SUB, 3, GH], BF16)

        self.consts_set, self.consts_made = sem("consts_set"), sem("consts_made")
        self.q_loaded = [sem("q_loaded0"), sem("q_loaded1")]
        self.k_loaded = [sem("k_loaded0"), sem("k_loaded1")]
        self.v_loaded = [sem("v_loaded0"), sem("v_loaded1")]
        self.piece_ready, self.piece_reduced = sem("piece_ready"), sem("piece_reduced")
        self.raw_ready, self.max_ready = sem("raw_ready"), sem("max_ready")
        self.hi_ready, self.rest_ready = sem("shift_hi_ready"), sem("shift_rest_ready")
        self.mid_ready, self.shift_ready = sem("shift_mid_ready"), sem("shift_ready")
        self.after_ready = sem("after_ready")
        self.parts_in = parts_d.rearrange("r (z b) (cc g h d) t -> r z (b cc) g d h t", b=B, cc=CC, g=2, h=GH)
        self.v_in = vpad_d.rearrange("(i g) p t f -> i g p t f", g=2)

    def set_constants(self, pool):
        pool.memset(self.ones[:], 1.0).then_inc(self.consts_set, 1)
        pool.memset(self.mask16[:], 0.0).then_inc(self.consts_set, 1)
        pool.memset(self.floor[:], 0.0).then_inc(self.consts_set, 1)
        pool.memset(self.after[:, NT - 1], 0.0).then_inc(self.consts_set, 1)
        pool.wait_ge(self.consts_set, 4)
        pool.memset(self.k_op[ROWS:KROWS], 1.0).then_inc(self.consts_set, 1)
        pool.wait_ge(self.consts_set, 5)
        pool.affine_select(out=self.keys_after[:], in_=self.ones[:], compare_op=ALU.is_gt, fill=0.0, base=0,
                           pattern=[[-1, P]], channel_multiplier=1).then_inc(self.consts_made, 1)
        pool.affine_select(out=self.mask16[:], in_=self.mask16[:], compare_op=ALU.is_ge, fill=NEG, base=0,
                           pattern=[[-1, P]], channel_multiplier=1).then_inc(self.consts_made, 1)
        pool.affine_select(out=self.floor[:, :, NT - 1], in_=self.floor[:, :, NT - 1], compare_op=ALU.not_equal, fill=LOWEST,
                           base=-(P - 1), pattern=[[0, GH]], channel_multiplier=1).then_inc(self.consts_made, 1)
        for half in range(2):
            counts = self.v_after[:, half].rearrange("p t (h w) -> p t h w", w=HW)[:, :, :, HD:HW]
            pool.iota(counts, pattern=[[-P, NT], [0, GH], [0, HW - HD]], base=T - 1, channel_multiplier=-1,
                      allow_small_or_imprecise_dtypes=True).then_inc(self.consts_made, 1)

    def load_group(self, sp, i, p):
        for r in range(len(Q_PARTS)):
            rows = slice(r * HD, (r + 1) * HD)
            sp.dma_start(self.q_op[rows, p], self.parts_in[Q_PARTS[r], 0, i, p]).then_inc(self.q_loaded[p], 16)
            sp.dma_start(self.k_op[rows, p], self.parts_in[K_PARTS[r], 1, i, p]).then_inc(self.k_loaded[p], 16)
        sp.dma_start(self.v_sb[:, p], self.v_in[i, p]).then_inc(self.v_loaded[p], 16)

    def add_up_after(self, pool, p, n, loads):
        pool.wait_ge(self.v_loaded[p], 16 * loads)
        values = self.v_sb[:, p].rearrange("p t (h w) -> p t h w", w=HW)
        for j in range(NT - 2, -1, -1):
            if j < NT - 2:
                pool.wait_ge(self.after_ready, n * (NT - 1) + NT - 2 - j)
            pool.tensor_tensor(self.after[:, j], self.after[:, j + 1], values[:, j + 1, :, 0:HD], ALU.add).then_inc(self.after_ready, 1)

    def score_piece(self, pe, ps_m, ring, f, p, base):
        u, h, s, pc, width = piece(f)
        pe.wait_ge(self.piece_reduced, base + (f + 1 + MRING - ring if f else MRING))
        q0 = u * CH + s * P
        last = pe.matmul(ps_m[:, f % ring, 0:width], self.q_op[0:ROWS, p, h, q0:q0 + P],
                         self.k_op[0:ROWS, p, h, pc * CH:pc * CH + width], start=True, stop=(pc < u))
        if pc == u:
            last = pe.matmul(ps_m[:, f % ring, s * P:width], self.ident16[:], self.mask16[:], start=False, stop=True)
        last.then_inc(self.piece_ready, 1)

    def reduce_piece(self, dve, ps_m, ring, f, base):
        u, h, s, pc, width = piece(f)
        dve.wait_ge(self.piece_ready, base + f + 1)
        dve.tensor_reduce(self.part_max[:, u % 2, h * SUB + s, pc:pc + 1], ps_m[:, f % ring, 0:width], AX_X,
                          ALU.max).then_inc(self.piece_reduced, 1)

    def max_step(self, dve, k, u, n, reduced):
        by_head = [self.shift[:, u, :, part].rearrange("p s h -> p h s") for part in range(3)]
        if k == 0:
            dve.wait_ge(self.piece_reduced, reduced + MRING)
            dve.tensor_reduce(self.raw_max[:].rearrange("p h s -> p (h s)"), self.part_max[:, u % 2, :, 0:u + 1], AX_X,
                              ALU.max).then_inc(self.raw_ready, 1)
        if k == 1:
            dve.wait_ge(self.raw_ready, n + 1)
            dve.tensor_tensor(self.row_max[:, u], self.raw_max[:], self.floor[:, :, u * SUB:(u + 1) * SUB],
                              ALU.max).then_inc(self.max_ready, 1)
        if k == 2:
            dve.wait_ge(self.max_ready, n + 1)
            dve.tensor_scalar(by_head[0], self.row_max[:, u], -1.0, None, ALU.mult).then_inc(self.hi_ready, 1)
        if k == 3:
            dve.wait_ge(self.hi_ready, n + 1)
            dve.scalar_tensor_tensor(self.shift_rest[:], self.row_max[:, u], -1.0, by_head[0], ALU.mult,
                                     ALU.subtract).then_inc(self.rest_ready, 1)
        if k == 4:
            dve.wait_ge(self.rest_ready, n + 1)
            dve.tensor_copy(by_head[1], self.shift_rest[:]).then_inc(self.mid_ready, 1)
        if k == 5:
            dve.wait_ge(self.mid_ready, n + 1)
            dve.tensor_tensor(by_head[2], self.shift_rest[:], by_head[1], ALU.subtract).then_inc(self.shift_ready, 1)

    def after_piece(self, dve, f, n0, base, close):
        for u in range(NCH):
            k = f + 1 - PIECE0[u + 1]
            if k == 0 and close:
                for step in range(MAX_STEPS):
                    self.max_step(dve, step, u, n0 + u, base + PIECE0[u + 1])
            elif 0 <= k < MAX_STEPS and not (u == NCH - 1 or close):
                self.max_step(dve, k, u, n0 + u, base + PIECE0[u + 1])


def stage_tokens(nc, x, w_in_t, w_r_t, w_k_t, w_v_t, w_out_t, mu_rk,
                 parts_d, vpad_d, ffn_d, ident, ident16, w_out_sb, consts_ready, ops):
    with ExitStack() as ctx:
        def sb(name, shape, dt=F32):
            return ctx.enter_context(nc.sbuf_tensor(name, shape, dt))

        def ps(name, shape):
            return ctx.enter_context(nc.psum_tensor(name, shape, F32))

        def sem(name):
            return ctx.enter_context(nc.semaphore(name))

        w_in_sb = sb("w_in_sb", [P, CC, 3 * C])
        w_r_sb = sb("w_r_sb", [P, CC, C])
        w_k_sb = sb("w_k_sb", [P, CC, C])
        w_v_sb = sb("w_v_sb", [P, CC, C])
        mu = sb("mu", [P, 2, CC])
        one_less_mu = sb("one_less_mu", [P, 2, CC])
        zeros = sb("zeros", [P, CC, 1])
        x_in = sb("x_in", [P, 2, SUB, C])
        stats = sb("stats", [P, SUB, 6])
        mean_var = sb("mean_var", [P, SUB, 2])
        var_eps = sb("var_eps", [P, SUB])
        root = sb("root", [P, SUB])
        inv_root = sb("inv_root", [P, SUB])
        fix = sb("fix", [P, SUB])
        rstd = sb("rstd", [P, SUB])
        xn = sb("xn", [P, SUB, C])
        xn_t = sb("xn_t", [P, CC, CH + 1])
        mixed = sb("mixed", [P, 2, CC, CH])
        prev_term = sb("prev_term", [P, 2, CC, CH])
        parts = sb("parts", [P, 2, 3, 2 * CC, CH], BF16)
        rest = sb("rest", [P, 2, CH])
        v_pad = sb("v_pad", [P, 2, SUB, H, HW])
        k_act = sb("k_act", [P, CC, CH])
        ffn = sb("ffn", [P, 2, SUB, C])

        ps_xt = ps("ps_xt", [P, CC, CH])
        ps_qk = ps("ps_qk", [P, 2, CH])
        ps_vr = ps("ps_vr", [P, 2, 2, C])
        ps_m = ps("ps_pieces", [P, 2, CH])

        w_in_loaded, weights_loaded, mu_loaded = sem("w_in_loaded"), sem("weights_loaded"), sem("mu_loaded")
        x_loaded = [sem("x_loaded0"), sem("x_loaded1")]
        parts_stored = [sem("parts_stored0"), sem("parts_stored1")]
        v_stored = [sem("v_stored0"), sem("v_stored1")]
        ffn_stored = [sem("ffn_stored0"), sem("ffn_stored1")]
        setup_done, mu_ready = sem("setup_done"), sem("mu_ready")
        stats_ready, aggr_ready, var_ready = sem("stats_ready"), sem("aggr_ready"), sem("var_ready")
        root_ready, newton, rstd_ready = sem("root_ready"), sem("newton"), sem("rstd_ready")
        xn_ready, xt_ready, halo_ready, xn_t_ready = sem("xn_ready"), sem("xt_ready"), sem("halo_ready"), sem("xn_t_ready")
        prev_ready, mixed_ready = sem("prev_ready"), sem("mixed_ready")
        qk_ready, hi_ready, rest_ready, mid_ready, parts_ready = (
            sem("qk_ready"), sem("hi_ready"), sem("rest_ready"), sem("mid_ready"), sem("parts_ready"))
        v_ready, v_pad_ready = sem("v_ready"), sem("v_pad_ready")
        r_ready, gate_ready = sem("r_ready"), sem("gate_ready")
        kt_ready, relu_ready, k_act_ready = sem("kt_ready"), sem("relu_ready"), sem("k_act_ready")
        o_ready, gated_ready, ffn_ready = sem("o_ready"), sem("gated_ready"), sem("ffn_ready")

        x_tiles = x.rearrange("(n s p) c -> n p s c", s=SUB, p=P)
        ffn_tiles = ffn_d.rearrange("(n s p) c -> n p s c", s=SUB, p=P)
        by_channel = "(cc p) n -> p cc n"
        passed = sem("passed")
        CREDIT = 16
        FREE = 2
        block = ctx.enter_context(nc.Block())

        @block.sync
        def _(sp):
            def batch(b, last):
                for c in range(NCH):
                    par = c % 2
                    n = b * NCH + c
                    if not (last and c == NCH - 1):
                        sp.wait_ge(ffn_ready, n * 2 + FREE)
                        sp.sem_inc(passed, 1)
                        sp.dma_start(x_in[:, 1 - par], x_tiles[n + 1]).then_inc(x_loaded[1 - par], 16)
                    if last and c == 0:
                        for i in range(2):
                            sp.wait_ge(parts_stored[i], CREDIT + b * (NCH // 2) * 96)
                            sp.wait_ge(v_stored[i], CREDIT + b * (NCH // 2) * SUB * 16)
                        ops.load_group(sp, 0, 0)
                    sp.wait_ge(v_pad_ready, (n + 1) * 2)
                    dst = vpad_d.rearrange("(b g) p t f -> b p t g f", b=B)
                    for s in range(SUB):
                        sp.dma_start(dst[b, :, c * SUB + s],
                                     v_pad[:, par, s].rearrange("p (g h) w -> p g (h w)", h=GH)).then_inc(v_stored[par], 16)
                    sp.wait_ge(parts_ready, (n + 1) * 4)
                    for part in range(3):
                        dst = parts_d[part].rearrange("(z b) (cc p) t -> b p z cc t", b=B, p=P)
                        for z in range(2):
                            sp.dma_start(dst[b, :, z, :, c * CH:(c + 1) * CH],
                                         parts[:, par, part, z * CC:(z + 1) * CC]).then_inc(parts_stored[par], 16)
                    sp.wait_ge(ffn_ready, n * 2 + 2 + FREE)
                    sp.dma_start(ffn_tiles[n], ffn[:, par]).then_inc(ffn_stored[par], 16)

            sp.dma_start(x_in[:, 0], x_tiles[0]).then_inc(x_loaded[0], 16)
            sp.dma_start(w_in_sb[:], w_in_t.rearrange(by_channel, p=P)).then_inc(w_in_loaded, 16)
            sp.dma_start(mu[:], mu_rk).then_inc(mu_loaded, 16)
            for w, w_sb in ((w_k_t, w_k_sb), (w_r_t, w_r_sb), (w_v_t, w_v_sb), (w_out_t, w_out_sb)):
                sp.dma_start(w_sb[:], w.rearrange(by_channel, p=P)).then_inc(weights_loaded, 16)
            for i in range(2):
                sp.sem_inc(parts_stored[i], CREDIT)
                sp.sem_inc(v_stored[i], CREDIT)
                sp.sem_inc(ffn_stored[i], CREDIT)
            sp.sem_inc(ffn_ready, FREE)
            sp.sem_inc(gate_ready, FREE)
            sp.sem_inc(gated_ready, FREE)
            sp.sem_inc(ops.piece_reduced, MRING)
            with sp.Fori(0, B - 1) as b:
                batch(b, False)
            batch(B - 1, True)
            for i in range(2):
                sp.wait_ge(parts_stored[i], CREDIT + NCH * 6 * 16)
                sp.wait_ge(v_stored[i], CREDIT + NCH * SUB * 16)
                sp.wait_ge(ffn_stored[i], CREDIT + NCH * 16)

        @block.gpsimd
        def _(pool):
            def batch(b, last):
                for c in range(NCH):
                    par = c % 2
                    n = b * NCH + c
                    if last and c == NCH - 1:
                        ops.add_up_after(pool, 0, 0, 1)
                    pool.wait_ge(relu_ready, n + 1)
                    pool.tensor_tensor(k_act[:], k_act[:], k_act[:], ALU.mult).then_inc(k_act_ready, 1)
                    for half in range(2):
                        tiles = slice(half * 2, half * 2 + 2)
                        pool.wait_ge(gated_ready, FREE + n * 2 + half + 1)
                        pool.tensor_tensor(ffn[:, par, tiles], ffn[:, par, tiles], x_in[:, par, tiles],
                                           ALU.add).then_inc(ffn_ready, 1)

            pool.memset(ident[:], 0.0).then_inc(setup_done, 1)
            pool.memset(zeros[:], 0.0).then_inc(setup_done, 1)
            pool.wait_ge(setup_done, 2)
            pool.affine_select(out=ident[:], in_=ident[:], compare_op=ALU.not_equal, fill=1.0, base=0,
                               pattern=[[-1, P]], channel_multiplier=1).then_inc(consts_ready, 1)
            pool.memset(v_pad[:, :, :, :, HD:HW], 1.0).then_inc(setup_done, 1)
            pool.memset(ident16[:], 0.0).then_inc(setup_done, 1)
            pool.wait_ge(setup_done, 4)
            pool.affine_select(out=ident16[:], in_=ident16[:], compare_op=ALU.not_equal, fill=1.0, base=0,
                               pattern=[[-1, P]], channel_multiplier=1).then_inc(consts_ready, 1)
            ops.set_constants(pool)
            with pool.Fori(0, B - 1) as b:
                batch(b, False)
            batch(B - 1, True)

        def token_stats(dve, n, par, loads):
            dve.wait_ge(x_loaded[par], 16 * loads)
            for s in range(SUB):
                dve.bn_stats(stats[:, s], x_in[:, par, s]).then_inc(stats_ready, 1)
            dve.wait_ge(stats_ready, n * SUB + SUB)
            dve.sem_inc(passed, 1)
            for s in range(SUB):
                dve.bn_aggr(mean_var[:, s], stats[:, s]).then_inc(aggr_ready, 1)
            dve.wait_ge(aggr_ready, n * SUB + SUB)
            dve.tensor_scalar(var_eps[:], mean_var[:, :, 1], EPS, None, ALU.add).then_inc(var_ready, 1)

        def normalise_tokens(dve, n, par):
            dve.wait_ge(root_ready, n + 1)
            dve.reciprocal(inv_root[:], root[:]).then_inc(newton, 1)
            dve.wait_ge(newton, n * 4 + 1)
            dve.tensor_tensor(fix[:], inv_root[:], inv_root[:], ALU.mult).then_inc(newton, 1)
            dve.wait_ge(newton, n * 4 + 2)
            dve.tensor_tensor(fix[:], fix[:], var_eps[:], ALU.mult).then_inc(newton, 1)
            dve.wait_ge(newton, n * 4 + 3)
            dve.tensor_scalar(fix[:], fix[:], -0.5, 1.5, ALU.mult, ALU.add).then_inc(newton, 1)
            dve.wait_ge(newton, n * 4 + 4)
            dve.tensor_tensor(rstd[:], inv_root[:], fix[:], ALU.mult).then_inc(rstd_ready, 1)
            dve.wait_ge(rstd_ready, n + 1)
            for s in range(SUB):
                dve.tensor_scalar(xn[:, s], x_in[:, par, s], mean_var[:, s, 0:1], rstd[:, s:s + 1],
                                  ALU.subtract, ALU.mult).then_inc(xn_ready, 1)

        @block.vector
        def _(dve):
            def prev_terms(z):
                for cc in range(CC):
                    dve.tensor_scalar(prev_term[:, z, cc], xn_t[:, cc, 0:CH], one_less_mu[:, z, cc:cc + 1],
                                      None, ALU.mult).then_inc(prev_ready, 1)

            def mix_tokens(n, z):
                for cc in range(CC):
                    dve.wait_ge(prev_ready, n * 4 + 2 * (1 - z) + cc + 1)
                    dve.scalar_tensor_tensor(mixed[:, z, cc], xn_t[:, cc, 1:CH + 1], mu[:, z, cc:cc + 1],
                                             prev_term[:, z, cc], ALU.mult, ALU.add).then_inc(mixed_ready, 1)

            def rest_of(n, par, j):
                dve.wait_ge(hi_ready, n * 4 + j + 1)
                dve.scalar_tensor_tensor(rest[:, j % 2], ps_qk[:, j % 2], SCALE if j < CC else 1.0,
                                         parts[:, par, 0, j], ALU.mult, ALU.subtract).then_inc(rest_ready, 1)

            def low_part(n, par, j):
                dve.wait_ge(mid_ready, n * 4 + j + 1)
                dve.tensor_tensor(parts[:, par, 2, j], rest[:, j % 2], parts[:, par, 1, j],
                                  ALU.subtract).then_inc(parts_ready, 1)

            def gate_half(n, par, half):
                dve.wait_ge(o_ready, n * 2 + half + 1)
                dve.wait_ge(gate_ready, FREE + n * 2 + half + 1)
                dve.tensor_tensor(ffn[:, par, half * 2:half * 2 + 2], ffn[:, par, half * 2:half * 2 + 2],
                                  ps_qk[:, half].rearrange("p (s c) -> p s c", c=C), ALU.mult).then_inc(gated_ready, 1)

            def batch(b, last):
                def pieces(c, step):
                    if last:
                        for f in pieces_beside_tokens(c, step):
                            ops.reduce_piece(dve, ps_m, 2, f, 0)
                            ops.after_piece(dve, f, 0, 0, False)

                for c in range(NCH):
                    par = c % 2
                    n = b * NCH + c
                    dve.wait_ge(xn_t_ready, n + 1)
                    prev_terms(1)
                    pieces(c, 0)
                    rest_of(n, par, 0)
                    prev_terms(0)
                    pieces(c, 1)
                    rest_of(n, par, 1)
                    low_part(n, par, 0)
                    mix_tokens(n, 1)
                    pieces(c, 2)
                    low_part(n, par, 1)
                    pieces(c, 3)
                    if not (last and c == NCH - 1):
                        token_stats(dve, n + 1, 1 - par, b * 2 + (c + 1) // 2 + 1)
                    rest_of(n, par, 2)
                    pieces(c, 4)
                    mix_tokens(n, 0)
                    rest_of(n, par, 3)
                    low_part(n, par, 2)
                    pieces(c, 5)
                    low_part(n, par, 3)
                    pieces(c, 6)
                    if not (last and c == NCH - 1):
                        normalise_tokens(dve, n + 1, 1 - par)
                    pieces(c, 7)
                    pieces(c, 8)
                    pieces(c, 9)
                    pieces(c, 10)
                    gate_half(n, par, 0)
                    pieces(c, 11)
                    gate_half(n, par, 1)
                if last:
                    for f in range(HEAD_START - PIECES_BEHIND, HEAD_START):
                        ops.reduce_piece(dve, ps_m, 2, f, 0)
                        ops.after_piece(dve, f, 0, 0, False)

            token_stats(dve, 0, 0, 1)
            normalise_tokens(dve, 0, 0)
            dve.wait_ge(mu_loaded, 16)
            dve.tensor_scalar(one_less_mu[:], mu[:], -1.0, 1.0, ALU.mult, ALU.add).then_inc(mu_ready, 1)
            dve.wait_ge(mu_ready, 1)
            with dve.Fori(0, B - 1) as b:
                batch(b, False)
            batch(B - 1, True)

        @block.scalar
        def _(act):
            def take_root(n):
                act.wait_ge(var_ready, n + 1)
                act.activation(root[:], var_eps[:], ACT.Sqrt).then_inc(root_ready, 1)

            def keep_tokens(n, first):
                act.wait_ge(xt_ready, n + 1)
                act.copy(xn_t[:, :, 0:1], zeros[:] if first else xn_t[:, :, CH:CH + 1]).then_inc(halo_ready, 1)
                act.wait_ge(halo_ready, n + 1)
                act.copy(xn_t[:, :, 1:CH + 1], ps_xt[:]).then_inc(xn_t_ready, 1)

            def high_part(n, par, j):
                act.wait_ge(qk_ready, n * 4 + j + 1)
                act.activation(parts[:, par, 0, j], ps_qk[:, j % 2], ACT.Copy,
                               scale=SCALE if j < CC else 1.0).then_inc(hi_ready, 1)

            def middle_part(n, par, j):
                act.wait_ge(rest_ready, n * 4 + j + 1)
                act.copy(parts[:, par, 1, j], rest[:, j % 2]).then_inc(mid_ready, 1)

            def keep_v(n, par, half):
                act.wait_ge(v_ready, n * 2 + half + 1)
                act.copy(v_pad[:, par, 2 * half:2 * half + 2, :, 0:HD],
                         ps_vr[:, half].rearrange("p s (h d) -> p s h d", d=HD)).then_inc(v_pad_ready, 1)

            def batch(b, last):
                for c in range(NCH):
                    par = c % 2
                    n = b * NCH + c
                    stores = b * 2 + c // 2
                    act.wait_ge(parts_stored[par], stores * 96 + CREDIT)
                    high_part(n, par, 0)
                    middle_part(n, par, 0)
                    high_part(n, par, 1)
                    act.wait_ge(v_stored[par], stores * (SUB * 16) + CREDIT)
                    keep_v(n, par, 0)
                    middle_part(n, par, 1)
                    keep_v(n, par, 1)
                    high_part(n, par, 2)
                    middle_part(n, par, 2)
                    high_part(n, par, 3)
                    if not (last and c == NCH - 1):
                        take_root(n + 1)
                    middle_part(n, par, 3)
                    act.wait_ge(kt_ready, n + 1)
                    act.activation(k_act[:], ps_xt[:], ACT.Relu).then_inc(relu_ready, 1)
                    act.wait_ge(ffn_stored[par], stores * 16 + CREDIT)
                    for half in range(2):
                        act.wait_ge(r_ready, n * 2 + half + 1)
                        act.activation(ffn[:, par, half * 2:half * 2 + 2], ps_vr[:, half], ACT.Sigmoid).then_inc(gate_ready, 1)
                    if not (last and c == NCH - 1):
                        keep_tokens(n + 1, c == NCH - 1)

            take_root(0)
            act.wait_ge(setup_done, 4)
            keep_tokens(0, True)
            with act.Fori(0, B - 1) as b:
                batch(b, False)
            batch(B - 1, True)

        @block.tensor
        def _(pe):
            def turn_tokens(n):
                pe.wait_ge(xn_ready, n * SUB + SUB)
                if not isinstance(n, int) or n > 0:
                    pe.wait_ge(relu_ready, n)
                for cc in range(CC):
                    for s in range(SUB):
                        last = pe.transpose(ps_xt[:, cc, s * P:(s + 1) * P], xn[:, s, cc * P:(cc + 1) * P], ident[:])
                last.then_inc(xt_ready, 1)

            def project_qk(n, j):
                if j >= 2:
                    pe.wait_ge(rest_ready, n * 4 + j - 1)
                else:
                    pe.wait_ge(gated_ready, n * 2 + j + 1)
                for cc in range(CC):
                    last = pe.matmul(ps_qk[:, j % 2], w_in_sb[:, cc, j * P:(j + 1) * P],
                                     xn_t[:, cc, 1:CH + 1], start=(cc == 0), stop=(cc == CC - 1))
                last.then_inc(qk_ready, 1)

            def two_tiles(psum, half, lhs, weights):
                for s in range(2):
                    for cc in range(CC):
                        t = half * 2 + s
                        last = pe.matmul(psum[:, s], lhs[:, cc, t * P:(t + 1) * P], weights[:, cc],
                                         start=(cc == 0), stop=(cc == CC - 1))
                return last

            def batch(b, last_batch):
                def pieces(c, step):
                    if last_batch:
                        for f in pieces_beside_tokens(c, step):
                            if f == 0:
                                pe.wait_ge(ops.consts_made, 3)
                                pe.wait_ge(ops.q_loaded[0], ops.LOADS)
                                pe.wait_ge(ops.k_loaded[0], ops.LOADS)
                            ops.score_piece(pe, ps_m, 2, f, 0, 0)

                for c in range(NCH):
                    n = b * NCH + c
                    pe.wait_ge(xn_t_ready, n + 1)
                    for j in range(2):
                        project_qk(n, j)
                        pieces(c, j)
                    for half in range(2):
                        pe.wait_ge(gate_ready, n * 2 + half + 1)
                        two_tiles(ps_vr[:, half], half, xn_t[:, :, 1:CH + 1], w_in_sb[:, :, 2 * C:3 * C]).then_inc(v_ready, 1)
                        pieces(c, 2 + half)
                    for j in range(2, 4):
                        project_qk(n, j)
                        pieces(c, 2 + j)
                    pe.wait_ge(weights_loaded, 16 * 4)
                    pe.wait_ge(mixed_ready, n * 4 + 2)
                    for m in range(CC):
                        for cc in range(CC):
                            last = pe.matmul(ps_xt[:, m], w_k_sb[:, cc, m * P:(m + 1) * P], mixed[:, 1, cc],
                                             start=(cc == 0), stop=(cc == CC - 1))
                        if m == CC - 1:
                            last.then_inc(kt_ready, 1)
                        pieces(c, 6 + m)
                    pe.wait_ge(mixed_ready, n * 4 + 4)
                    for half in range(2):
                        pe.wait_ge(v_pad_ready, n * 2 + half + 1)
                        two_tiles(ps_vr[:, half], half, mixed[:, 0], w_r_sb).then_inc(r_ready, 1)
                        pieces(c, 8 + half)
                    if not (last_batch and c == NCH - 1):
                        turn_tokens(n + 1)
                    pe.wait_ge(k_act_ready, n + 1)
                    for half in range(2):
                        pe.wait_ge(parts_ready, n * 4 + 3 + half)
                        two_tiles(ps_qk[:, half].rearrange("p (s c) -> p s c", c=C), half, k_act,
                                  w_v_sb).then_inc(o_ready, 1)
                        pieces(c, 10 + half)
                if last_batch:
                    for f in range(HEAD_START - PIECES_BEHIND, HEAD_START):
                        ops.score_piece(pe, ps_m, 2, f, 0, 0)

            pe.wait_ge(consts_ready, 1)
            turn_tokens(0)
            pe.wait_ge(w_in_loaded, 16)
            with pe.Fori(0, B - 1) as b:
                batch(b, False)
            batch(B - 1, True)


def stage_attention(nc, ops, ident, ident16, attn_t, ffn_d, w_out_sb, out):
    with ExitStack() as ctx:
        def sb(name, shape, dt=F32):
            return ctx.enter_context(nc.sbuf_tensor(name, shape, dt))

        def ps(name, shape):
            return ctx.enter_context(nc.psum_tensor(name, shape, F32))

        def sem(name):
            return ctx.enter_context(nc.semaphore(name))

        probs = sb("probs", [P, PRING, CH])
        shift_t = sb("shift_t", [3 * GH, 2, CH], BF16)
        masked_weight = sb("masked_weight", [P, NCH, GH * SUB])
        diag_weight = sb("diag_weight", [P, 2, GH * SUB, P])
        sums = sb("sums", [P, 2, CH])
        turned = sb("turned", [P, CH])
        inv_denom = sb("inv_denom", [P, CH // HW])
        normed = sb("normed", [P, 2, CH])

        ps_s = ps("ps_s", [P, SRING, CH])
        ps_m = ps("ps_m", [P, MRING, CH])
        ps_o = ps("ps_o", [P, CH])
        ps_x = ps("ps_x", [P, CH])
        ps_shift = ps_x[:].bitcast(BF16)

        shift_turned, shift_t_ready = sem("shift_turned"), sem("shift_t_ready")
        shift_loaded = [sem("shift_loaded0"), sem("shift_loaded1")]
        weight_ready, diag_ready = sem("weight_ready"), sem("diag_ready")
        suffix_ready, v_after_ready = sem("suffix_ready"), sem("v_after_ready")
        scores_ready, probs_ready, probs_masked, probs_used = (
            sem("scores_ready"), sem("probs_ready"), sem("probs_masked"), sem("probs_used"))
        out_ready, sums_ready, turned_ready, denom_ready, divided, normed_ready = (
            sem("out_ready"), sem("sums_ready"), sem("turned_ready"), sem("denom_ready"),
            sem("divided"), sem("normed_ready"))
        normed_stored = [sem("normed_stored0"), sem("normed_stored1")]
        ffn_loaded = [sem(f"ffn_loaded{k}") for k in range(ORING)]
        out_stored = [sem(f"out_stored{k}") for k in range(ORING)]
        y_ready, total_ready = sem("y_ready"), sem("total_ready")
        ffn_tiles = ffn_d.rearrange("(n s p) c -> n p s c", s=SUB, p=P)
        out_tiles = out.rearrange("(n s p) c -> n p s c", s=SUB, p=P)
        passed = sem("passed_mask")
        SHIFTS = 3 * 16
        STORES = GH * 16
        USED = PRING // GH
        q_op, k_op, v_sb, after, v_after = ops.q_op, ops.k_op, ops.v_sb, ops.after, ops.v_after
        keys_after, ones, row_max, shift = ops.keys_after, ops.ones, ops.row_max, ops.shift
        q_loaded, k_loaded, after_ready, max_ready, shift_ready = (
            ops.q_loaded, ops.k_loaded, ops.after_ready, ops.max_ready, ops.shift_ready)
        total = [buf[:, 0, half * 8:half * 8 + 8].rearrange("p (s a) f -> p s (a f)", s=SUB)
                 for buf in (v_sb, v_after) for half in range(ORING // 2)]
        block = ctx.enter_context(nc.Block())

        def unit_of(i, p, u):
            return (i * 2 + p) * NCH + u

        @block.sync
        def _(sp):
            def place_shift(p, u, n):
                sp.wait_ge(shift_t_ready, n + 1)
                for part in range(3):
                    sp.dma_start(q_op[ROWS + part:ROWS + part + 1, p, :, u * CH:(u + 1) * CH],
                                 shift_t[part * GH:(part + 1) * GH, u % 2]).then_inc(shift_loaded[u % 2], 16)

            def keep_normed(i, p, u):
                sp.wait_ge(normed_ready, unit_of(i, p, u) + 3)
                for h in range(GH):
                    row = (p * GH + h) * HD
                    sp.dma_start(attn_t[row:row + HD, i, u * CH:(u + 1) * CH],
                                 normed[h * HW:h * HW + HD, u % 2]).then_inc(normed_stored[u % 2], 16)

            def store_chunk(n):
                sp.wait_ge(total_ready, SUB * (n + 1))
                sp.dma_start(out_tiles[n], total[n % ORING]).then_inc(out_stored[n % ORING], 16)

            def group(i, p, first=False, last=False):
                if not first:
                    keep_normed(i - 1 + p, 1 - p, NCH - 1)
                if not last:
                    sp.wait_ge(out_ready, unit_of(i, p, 0) + 1)
                    ops.load_group(sp, i + p, 1 - p)
                place_shift(p, 2, unit_of(i, p, 2))
                keep_normed(i, p, 0)
                keep_normed(i, p, 1)
                place_shift(p, 3, unit_of(i, p, 3))
                if last:
                    store_chunk(0)
                keep_normed(i, p, 2)
                if not last:
                    place_shift(1 - p, 0, unit_of(i, p, NCH))
                    place_shift(1 - p, 1, unit_of(i, p, NCH + 1))
                if last:
                    for n in range(1, OUT_CHUNKS):
                        store_chunk(n)
                    keep_normed(i, p, NCH - 1)
                    for n in range(OUT_CHUNKS, B * NCH):
                        store_chunk(n)

            sp.sem_inc(probs_ready, SRING)
            sp.sem_inc(probs_used, USED)
            sp.sem_inc(out_ready, 1)
            sp.sem_inc(sums_ready, 1)
            sp.sem_inc(normed_ready, 2)
            for half in range(2):
                sp.sem_inc(normed_stored[half], STORES)
                sp.sem_inc(shift_loaded[half], SHIFTS)
            place_shift(0, 0, 0)
            place_shift(0, 1, 1)
            group(0, 0, first=True)
            with sp.Fori(0, B * CC - 1) as i:
                group(i, 1)
                group(i + 1, 0)
            group(B * CC - 1, 1, last=True)
            for s in normed_stored:
                sp.wait_ge(s, STORES * (1 + B * NG * NCH // 2))
            for s in out_stored:
                sp.wait_ge(s, 16 * (B * NCH // ORING))

        @block.gpsimd
        def _(pool):
            def spread_weight(u, n):
                pool.wait_ge(weight_ready, n + 1)
                if not isinstance(n, int) or n > 0:
                    pool.wait_ge(out_ready, n)
                pool.tensor_tensor(diag_weight[:, u % 2], ident[:].unsqueeze(1).broadcast_to([P, GH * SUB, P]),
                                   masked_weight[:, u].unsqueeze(2).broadcast_to([P, GH * SUB, P]),
                                   ALU.mult).then_inc(diag_ready, 1)

            def load_chunk(n):
                if n >= ORING:
                    pool.wait_ge(out_stored[n % ORING], 16 * (n // ORING))
                pool.dma_start(total[n % ORING], ffn_tiles[n]).then_inc(ffn_loaded[n % ORING], 16)

            def group(i, p, first=False, last=False):
                G = i * 2 + p
                for u in range(NCH):
                    if u == 2 and not last:
                        pool.wait_ge(v_after_ready, G * 4 + 4)
                        ops.add_up_after(pool, 1 - p, G + 1, i + 1 + p)
                    if last and u == 1:
                        pool.wait_ge(out_ready, unit_of(i, p, 0) + 1)
                        for n in range(ORING):
                            load_chunk(n)
                    if last and u == NCH - 1:
                        for n in range(ORING, B * NCH - 1):
                            load_chunk(n)
                    if u == NCH - 1 and not last:
                        spread_weight(0, unit_of(i, p, NCH))
                    for kt in range(SUB * u, SUB * u + SUB):
                        for h in range(GH):
                            slot = (KT0[u] + kt) * GH + h
                            pool.wait_ge(probs_ready, G * SLOTS + slot + 1 + SRING)
                            pool.sem_inc(passed, 1)
                            blk = probs[:, slot % PRING, 0:P]
                            pool.affine_select(out=blk, in_=blk, compare_op=ALU.is_ge, fill=0.0, base=0,
                                               pattern=[[1, P]], channel_multiplier=-1).then_inc(probs_masked, 1)
                    if last and u == NCH - 1:
                        load_chunk(B * NCH - 1)
                    if u < NCH - 1:
                        spread_weight(u + 1, unit_of(i, p, u + 1))

            spread_weight(0, 0)
            group(0, 0, first=True)
            with pool.Fori(0, B * CC - 1) as i:
                group(i, 1)
                group(i + 1, 0)
            group(B * CC - 1, 1, last=True)

        @block.scalar
        def _(act):
            def weight(n, u):
                act.wait_ge(max_ready, n + 1)
                act.activation(masked_weight[:, u], row_max[:, u].rearrange("p h s -> p (h s)"), ACT.Exp,
                               scale=-1.0).then_inc(weight_ready, 1)

            def keep_suffix(p, quad, n):
                act.wait_ge(suffix_ready, n + 1)
                act.copy(v_after[:, p, quad * SUB:(quad + 1) * SUB].rearrange("p s (h w) -> p (s h) w", w=HW)[:, :, 0:HD],
                         ps_x[:, 0:SUB * GH * HD].rearrange("p (f d) -> p f d", d=HD)).then_inc(v_after_ready, 1)

            def keep_shift(u, n, earlier):
                act.wait_ge(shift_turned, n + 1)
                act.wait_ge(shift_loaded[u % 2], (earlier + 1) * SHIFTS)
                act.copy(shift_t[:, u % 2], ps_shift[0:3 * GH, 0:CH]).then_inc(shift_t_ready, 1)

            def keep_sums(n, par):
                act.wait_ge(out_ready, n + 2)
                act.wait_ge(normed_ready, n + 1)
                act.copy(sums[:, par], ps_o[:]).then_inc(sums_ready, 1)

            def group(i, p, first=False, last=False):
                G = i * 2 + p
                for u in range(NCH):
                    nxt = NCH if u == NCH - 1 else 0
                    for kt in range(key_tiles(u)):
                        width = CH - first_query(u, kt)
                        act.wait_ge(probs_used, G * KTILES + KT0[u] + kt + 1)
                        for h in range(GH):
                            slot = (KT0[u] + kt) * GH + h
                            act.wait_ge(scores_ready, G * SLOTS + slot + 1)
                            act.activation(probs[:, slot % PRING, 0:width], ps_s[:, slot % SRING, 0:width],
                                           ACT.Exp).then_inc(probs_ready, 1)
                        if kt == LAG - 1 and not (first and u == 0):
                            keep_sums(unit_of(i, p, u - 1), (u - 1) % 2)
                        if first and (u, kt) in FIRST_SV_AT:
                            keep_suffix(0, FIRST_SV_AT[u, kt], FIRST_SV_AT[u, kt])
                        if (u, kt) in SV_AT and not last:
                            keep_suffix(1 - p, SV_AT[u, kt], (G + 1) * 4 + SV_AT[u, kt])
                        if (u, kt) in SHIFT_AT and not (nxt and last):
                            v = SHIFT_AT[u, kt]
                            weight(unit_of(i, p, v + nxt), v)
                            keep_shift(v, unit_of(i, p, v + nxt), (G + (nxt > 0)) * (NCH // 2) + v // 2)
                if last:
                    keep_sums(unit_of(i, p, NCH - 1), 1)

            for u in range(2):
                keep_shift(u, u, 0)
            for u in range(2):
                weight(u, u)
            group(0, 0, first=True)
            with act.Fori(0, B * CC - 1) as i:
                group(i, 1)
                group(i + 1, 0)
            group(B * CC - 1, 1, last=True)

        @block.vector
        def _(dve):
            def norm_step(k, n, par, stored):
                blocks = turned[:].rearrange("p (b w) -> p b w", w=HW)
                if k == 0:
                    dve.wait_ge(normed_ready, n + 2)
                    dve.wait_ge(sums_ready, n + 2)
                    dve.transpose(turned[:], sums[:, par]).then_inc(turned_ready, 1)
                if k == 1:
                    dve.wait_ge(turned_ready, n + 1)
                    dve.reciprocal(inv_denom[:], blocks[:, :, HD]).then_inc(denom_ready, 1)
                if k == 2:
                    dve.wait_ge(denom_ready, n + 1)
                    dve.tensor_tensor(blocks[:, :, 0:HD], blocks[:, :, 0:HD],
                                      inv_denom[:].unsqueeze(2).broadcast_to([P, CH // HW, HD]), ALU.mult).then_inc(divided, 1)
                if k == 3:
                    dve.wait_ge(divided, n + 1)
                    dve.wait_ge(normed_stored[par], (stored + 1) * STORES)
                    dve.transpose(normed[:, par], turned[:]).then_inc(normed_ready, 1)

            def add_tile(k):
                n, t = divmod(k, SUB)
                dve.wait_ge(ffn_loaded[n % ORING], 16 * (n // ORING + 1))
                dve.wait_ge(y_ready, k + 1)
                dve.tensor_tensor(total[n % ORING][:, t], total[n % ORING][:, t], ps_m[:, k % MRING, 0:C],
                                  ALU.add).then_inc(total_ready, 1)

            def group(i, p, first=False, last=False):
                G = i * 2 + p
                for u in range(NCH):
                    nxt = NCH if u == NCH - 1 else 0
                    base = (G + (nxt > 0)) * PIECES
                    for hs in range(key_tiles(u) * GH):
                        if not (nxt and last):
                            for f in pieces_of(u, hs):
                                ops.reduce_piece(dve, ps_m, MRING, f, base)
                                ops.after_piece(dve, f, unit_of(i, p, nxt), base, f + 1 == PIECES)
                        if NORM_AT <= hs < NORM_AT + NORM_STEPS and not (first and u == 0):
                            norm_step(hs - NORM_AT, unit_of(i, p, u - 1), (u - 1) % 2,
                                      G * (NCH // 2) + (u - 1) // 2)
                        if last and hs % GH == GH - 1 and (u, hs // GH) in OUT_AT:
                            add_tile(OUT_AT[u, hs // GH])
                if last:
                    for k in range(NORM_STEPS):
                        norm_step(k, unit_of(i, p, NCH - 1), 1, G * (NCH // 2) + (NCH - 1) // 2)
                    for k in range(len(OUT_AT), OUTS):
                        add_tile(k)

            group(0, 0, first=True)
            with dve.Fori(0, B * CC - 1) as i:
                group(i, 1)
                group(i + 1, 0)
            group(B * CC - 1, 1, last=True)

        @block.tensor
        def _(pe):
            def turn_shift(u, n, quads):
                pe.wait_ge(shift_ready, n + 1)
                if not isinstance(n, int) or n > 0:
                    pe.wait_ge(shift_t_ready, n)
                if not isinstance(quads, int) or quads > 0:
                    pe.wait_ge(v_after_ready, quads)
                for s in range(SUB):
                    last = pe.transpose(ps_shift[0:3 * GH, s * P:(s + 1) * P],
                                        shift[:, u, s].rearrange("p r h -> p (r h)"), ident16[:])
                last.then_inc(shift_turned, 1)

            def sum_suffix(p, quad, n, turned_before):
                pe.wait_ge(after_ready, (n + 1) * (NT - 1))
                if not isinstance(n, int) or quad > 0:
                    pe.wait_ge(v_after_ready, n * 4 + quad)
                if not isinstance(turned_before, int) or turned_before > 0:
                    pe.wait_ge(shift_t_ready, turned_before)
                tiles = slice(quad * SUB, (quad + 1) * SUB)
                values = v_sb[:, p, tiles].rearrange("p s (h w) -> p (s h) w", w=HW)[:, :, 0:HD]
                width = SUB * GH * HD
                pe.matmul(ps_x[:, 0:width], keys_after[:], values, start=True, stop=False)
                pe.matmul(ps_x[:, 0:width], ones[:], after[:, tiles].rearrange("p s h d -> p (s h d)"),
                          start=False, stop=True).then_inc(suffix_ready, 1)

            def score_tile(p, u, kt, h, G):
                slot = (KT0[u] + kt) * GH + h
                q0 = first_query(u, kt)
                pe.wait_ge(probs_ready, G * SLOTS + (slot + 1 if slot else SRING))
                pe.matmul(ps_s[:, slot % SRING, 0:CH - q0], k_op[0:KROWS, p, h, kt * P:(kt + 1) * P],
                          q_op[0:KROWS, p, h, u * CH + q0:(u + 1) * CH], start=True, stop=True).then_inc(scores_ready, 1)

            def weigh_values(p, u, kt, G):
                n = G * NCH + u
                if kt == 0:
                    pe.wait_ge(sums_ready, n + 1)
                if kt < SUB * u:
                    pe.wait_ge(probs_ready, G * SLOTS + (KT0[u] + kt + 1) * GH + SRING)
                else:
                    pe.wait_ge(probs_masked, n * (SUB * GH) + (kt - SUB * u + 1) * GH)
                q0 = first_query(u, kt)
                for h in range(GH):
                    last = pe.matmul(ps_o[h * HW:(h + 1) * HW, q0:CH], v_sb[:, p, kt, h * HW:(h + 1) * HW],
                                     probs[:, ((KT0[u] + kt) * GH + h) % PRING, 0:CH - q0], start=(kt == 0), stop=False)
                last.then_inc(probs_used, 1)

            def masked_keys(p, u, G):
                pe.wait_ge(diag_ready, G * NCH + u + 1)
                pe.wait_ge(v_after_ready, G * 4 + 4)
                for s in range(SUB):
                    for h in range(GH):
                        last = pe.matmul(ps_o[h * HW:(h + 1) * HW, s * P:(s + 1) * P],
                                         v_after[:, p, u * SUB + s, h * HW:(h + 1) * HW],
                                         diag_weight[:, u % 2, h * SUB + s], start=False, stop=(s == SUB - 1))
                last.then_inc(out_ready, 1)

            def finish_unit(p, u, G, step):
                weigh_values(p, u, key_tiles(u) - LAG + step, G)
                if step == LAG - 1:
                    masked_keys(p, u, G)

            def output_tile(k):
                n, t = divmod(k, SUB)
                b, c = divmod(n, NCH)
                if k < MRING:
                    pe.wait_ge(ops.piece_reduced, B * NG * PIECES + MRING)
                else:
                    pe.wait_ge(total_ready, k + 1 - MRING)
                pe.wait_ge(normed_stored[c % 2], ((b + 1) * NG * (NCH // 2) - (NCH // 2 - 1 - c // 2) + 1) * STORES)
                for cc in range(CC):
                    last = pe.matmul(ps_m[:, k % MRING, 0:C], attn_t[:, b * CC + cc, c * CH + t * P:c * CH + (t + 1) * P],
                                     w_out_sb[:, cc], start=(cc == 0), stop=(cc == CC - 1))
                last.then_inc(y_ready, 1)

            def group(i, p, first=False, last=False):
                G = i * 2 + p
                pe.wait_ge(q_loaded[p], (i + 1) * ops.LOADS)
                pe.wait_ge(k_loaded[p], (i + 1) * ops.LOADS)
                for u in range(NCH):
                    nxt = NCH if u == NCH - 1 else 0
                    pe.wait_ge(shift_loaded[u % 2], (G * (NCH // 2) + u // 2 + 2) * SHIFTS)
                    if nxt and not last:
                        pe.wait_ge(q_loaded[1 - p], (i + 1 + p) * ops.LOADS)
                        pe.wait_ge(k_loaded[1 - p], (i + 1 + p) * ops.LOADS)
                    for kt in range(key_tiles(u)):
                        for h in range(GH):
                            score_tile(p, u, kt, h, G)
                            if not (nxt and last):
                                for f in pieces_of(u, kt * GH + h):
                                    ops.score_piece(pe, ps_m, MRING, f, 1 - p if nxt else p, (G + (nxt > 0)) * PIECES)
                            if h == 2:
                                if kt >= LAG:
                                    weigh_values(p, u, kt - LAG, G)
                                elif u > 0:
                                    finish_unit(p, u - 1, G, kt)
                                elif not first:
                                    finish_unit(1 - p, NCH - 1, G - 1, kt)
                        if last and (u, kt) in OUT_AT:
                            output_tile(OUT_AT[u, kt])
                        if first and (u, kt) in FIRST_SV_AT:
                            sum_suffix(0, FIRST_SV_AT[u, kt], 0, 2)
                        if (u, kt) in SV_AT and not last:
                            sum_suffix(1 - p, SV_AT[u, kt], G + 1,
                                       unit_of(i, p, NCH + sum(a == u and b < kt for a, b in SHIFT_AT)))
                        if (u, kt) in SHIFT_AT and not (nxt and last):
                            v = SHIFT_AT[u, kt]
                            quads = (G + 1) * 4 + (sum(b < kt for _, b in SV_AT) if nxt else 0)
                            turn_shift(v, unit_of(i, p, v + nxt), quads)
                if last:
                    for step in range(LAG):
                        finish_unit(p, NCH - 1, G, step)
                    for k in range(len(OUT_AT), OUTS):
                        output_tile(k)

            for u in range(2):
                turn_shift(u, u, 0)
            group(0, 0, first=True)
            with pe.Fori(0, B * CC - 1) as i:
                group(i, 1)
                group(i + 1, 0)
            group(B * CC - 1, 1, last=True)


def kernel(L0_attn_x, L0_attn_w_in, L0_attn_w_out, L0_ffn_W_r, L0_ffn_W_k, L0_ffn_W_v, L0_ffn_mu_r, L0_ffn_mu_k):
    import numpy as np
    import concourse.bacc as bacc
    from concourse.bass_utils import run_bass_kernel_spmd

    def laid(a, turn=False):
        a = np.asarray(a)
        return np.ascontiguousarray(a.T if turn else a)

    inputs = {
        "x": laid(L0_attn_x).reshape(B * T, C),
        "w_in_t": laid(L0_attn_w_in, True),
        "w_r_t": laid(L0_ffn_W_r, True),
        "w_k_t": laid(L0_ffn_W_k, True),
        "w_v_t": laid(L0_ffn_W_v, True),
        "w_out_t": laid(L0_attn_w_out, True),
        "mu_rk": laid(np.stack([np.asarray(L0_ffn_mu_r), np.asarray(L0_ffn_mu_k)]).reshape(2, CC, P).transpose(2, 0, 1)),
    }
    nc = bacc.Bacc("TRN2", target_bir_lowering=False, num_devices=1)
    nc.disable_value_cache = True
    args = [nc.dram_tensor(name, a.shape, F32, kind="ExternalInput").ap() for name, a in inputs.items()]
    y = nc.dram_tensor("y", (B * T, C), F32, kind="ExternalOutput").ap()
    build(nc, *args, y)
    r = run_bass_kernel_spmd(nc, [inputs], core_ids=[0])
    return r.results[0]["y"].reshape(B, T, C)
```
